# Optimizing a Trainium2 kernel written in Bass

```python
import numpy as np
import jax
import jax.numpy as jnp

def _softmax(x, axis=-1):
    return jax.nn.softmax(x, axis=axis)

def _gelu(x):
    return jax.nn.gelu(x, approximate=True)

def _silu(x):
    return jax.nn.silu(x)

def _sigmoid(x):
    return jax.nn.sigmoid(x)

def _layernorm(x, axis=-1, eps=1e-05):
    m = jnp.mean(x, axis=axis, keepdims=True)
    v = jnp.var(x, axis=axis, keepdims=True)
    return (x - m) / jnp.sqrt(v + eps)

def _scatter_add(tgt, idx, src, axis=0):
    return tgt.at[idx].add(src)

def _segment_sum(src, seg, n):
    return jax.ops.segment_sum(src, seg, n)
kernel_name = 'mk_gnn_preln_d4_gnn_r32_e6111d'

def setup_inputs(seed: int=0):
    np.random.seed(seed)
    _w = jnp.asarray

    def _rec_inputs():
        import jax
        import jax.numpy as jnp
        _gk = jax.random.key(seed)
        x = -0.0005121 + 1.001 * jax.random.normal(jax.random.fold_in(_gk, 1), (3125, 160), jnp.float32)
        src = jax.random.randint(jax.random.fold_in(_gk, 2), (100000,), 0, 3125, jnp.int32)
        dst = jnp.minimum((3125 * jax.random.uniform(jax.random.fold_in(_gk, 3), (100000,)) ** 2.0).astype(jnp.int32), 99999)
        _o = jnp.argsort(dst, stable=True)
        src = src[_o]
        dst = dst[_o]
        edge_attr_4 = 0.000735704 + 1.0001 * jax.random.normal(jax.random.fold_in(_gk, 12), (100000, 4), jnp.float32)
        edge_attr_64 = 0.000127647 + 1.00004 * jax.random.normal(jax.random.fold_in(_gk, 13), (100000, 64), jnp.float32)
        node_vec1 = -0.00719938 + 0.999885 * jax.random.normal(jax.random.fold_in(_gk, 15), (3125, 1), jnp.float32)
        return (x, src, dst, edge_attr_4, edge_attr_64, node_vec1)
    x, src, dst, edge_attr_4, edge_attr_64, node_vec1 = _rec_inputs()

    def _L0_gnn_setup():
        import jax, jax.numpy as jnp
        import numpy as np
        N = 625
        E = 20000
        INV_SQRT3 = 0.5773502691896258
        INV8 = 0.125
        INV_SQRT32 = 0.17677669529663687
        INV64 = 0.015625
        INV32 = 0.03125
        INV_SQRT2048 = 0.022097086912079608
        key = jax.random.key(seed)
        ks = jax.random.split(key, 16)
        f32 = jnp.float32
        return {'node_features': jax.random.normal(ks[0], (N, 160), f32), 'edge_index': jax.random.randint(ks[1], (2, E), 0, N), 'edge_attr_tensor': jax.random.normal(ks[2], (E, 4), f32), 'node_attr_scalar_raw': jax.random.normal(ks[3], (N, 1), f32), 'Wm_ss': jax.random.normal(ks[4], (64, 64), f32), 'Wm_vv': jax.random.normal(ks[5], (32, 64), f32), 'Wm_sv': jax.random.normal(ks[6], (64, 32), f32), 'Wm_vs': jax.random.normal(ks[7], (32, 32), f32), 'Lm_s': jax.random.normal(ks[8], (64, 64), f32), 'Lm_v': jax.random.normal(ks[9], (32, 32), f32), 'Wu_ss': jax.random.normal(ks[10], (64, 64, 64), f32), 'Wu_vv': jax.random.normal(ks[11], (32, 32, 64), f32), 'Wu_sv': jax.random.normal(ks[12], (64, 32, 32), f32), 'Wu_vs': jax.random.normal(ks[13], (32, 64, 32), f32), 'Lu_s': jax.random.normal(ks[14], (64, 64), f32), 'Lu_v': jax.random.normal(ks[15], (32, 32), f32)}
    _L0_gnn_all = _L0_gnn_setup()
    _L0_gnn_in = {k: v for k, v in _L0_gnn_all.items() if k in ('Wm_ss', 'Wm_vv', 'Wm_sv', 'Wm_vs', 'Lm_s', 'Lm_v', 'Wu_ss', 'Wu_vv', 'Wu_sv', 'Wu_vs', 'Lu_s', 'Lu_v')}
    del _L0_gnn_all

    def _L1_gnn_setup():
        import jax, jax.numpy as jnp
        import numpy as np
        N, E = (1250, 20000)
        S_IN, V_IN = (64, 32)
        S_MID, V_MID = (96, 128)
        S_OUT, V_OUT = (96, 32)
        R = 64
        FC_HID = 64
        W_NUMEL = 64 + 64 + 32 + 32 + 32
        NUM_NEIGHBORS = 16.0

        def _inv(d):
            return 1.0 / jnp.sqrt(jnp.float32(d))

        def _forward(node_features, node_attr, edge_attr, edge_scalars, lin1_ws, lin1_wv, fc_w1, fc_w2, sc_ws, sc_wv, lin2_ws, lin2_wv, edge_src, edge_dst):
            n = node_features.shape[0]
            s = node_features[:, :S_IN]
            v = node_features[:, S_IN:].reshape(n, V_IN, 3)
            a = node_attr
            sc_s = s @ sc_ws * a * _inv(S_IN)
            sc_v = jnp.einsum('nci,cd->ndi', v, sc_wv) * a[:, :, None] * _inv(V_IN)
            h_s = s @ lin1_ws * a * _inv(S_IN)
            h_v = jnp.einsum('nci,cd->ndi', v, lin1_wv) * a[:, :, None] * _inv(V_IN)
            hid = jax.nn.silu(edge_scalars @ fc_w1 * _inv(R))
            w = hid @ fc_w2 * _inv(FC_HID)
            w1, w2, w3, w4, w5 = jnp.split(w, [64, 128, 160, 192], axis=-1)
            es = h_s[edge_src]
            ev = h_v[edge_src]
            e0 = edge_attr[:, :1]
            e1 = edge_attr[:, 1:4]
            m_s1 = w1 * es * e0
            m_s2 = w4 * jnp.einsum('eci,ei->ec', ev, e1) * _inv(3)
            m_v1 = (w2 * es)[:, :, None] * e1[:, None, :]
            m_v2 = w3[:, :, None] * ev * e0[:, :, None]
            m_v3 = w5[:, :, None] * jnp.cross(ev, e1[:, None, :]) * _inv(2)
            mid_s = jnp.concatenate([m_s1, m_s2], axis=-1)
            mid_v = jnp.concatenate([m_v1, m_v2, m_v3], axis=1)
            inv_nn = 1.0 / jnp.sqrt(jnp.float32(NUM_NEIGHBORS))
            agg_s = jax.ops.segment_sum(mid_s, edge_dst, num_segments=n) * inv_nn
            agg_v = jax.ops.segment_sum(mid_v, edge_dst, num_segments=n) * inv_nn
            o_s = agg_s @ lin2_ws * a * _inv(S_MID)
            o_v = jnp.einsum('nci,cd->ndi', agg_v, lin2_wv) * a[:, :, None] * _inv(V_MID)
            pre_s = sc_s + o_s
            pre_v = sc_v + o_v
            scalars = jax.nn.silu(pre_s[:, :64])
            gates = jax.nn.sigmoid(pre_s[:, 64:96])
            gated = gates[:, :, None] * pre_v
            return jnp.concatenate([scalars, gated.reshape(n, 3 * V_OUT)], axis=-1)
        key = jax.random.key(seed)
        ks = jax.random.split(key, 13)
        return {'node_features': jax.random.normal(ks[0], (N, S_IN + 3 * V_IN), jnp.float32), 'node_attr': jnp.ones((N, 1), jnp.float32), 'edge_src': jax.random.randint(ks[1], (E,), 0, N), 'edge_dst': jax.random.randint(ks[2], (E,), 0, N), 'edge_attr': jax.random.normal(ks[3], (E, 4), jnp.float32), 'edge_scalars': jax.random.normal(ks[4], (E, R), jnp.float32), 'lin1_ws': jax.random.normal(ks[5], (S_IN, S_IN), jnp.float32), 'lin1_wv': jax.random.normal(ks[6], (V_IN, V_IN), jnp.float32), 'fc_w1': jax.random.normal(ks[7], (R, FC_HID), jnp.float32), 'fc_w2': jax.random.normal(ks[8], (FC_HID, W_NUMEL), jnp.float32), 'sc_ws': jax.random.normal(ks[9], (S_IN, S_OUT), jnp.float32), 'sc_wv': jax.random.normal(ks[10], (V_IN, V_OUT), jnp.float32), 'lin2_ws': jax.random.normal(ks[11], (S_MID, S_OUT), jnp.float32), 'lin2_wv': jax.random.normal(ks[12], (V_MID, V_OUT), jnp.float32)}
    _L1_gnn_all = _L1_gnn_setup()
    _L1_gnn_in = {k: v for k, v in _L1_gnn_all.items() if k in ('lin1_ws', 'lin1_wv', 'fc_w1', 'fc_w2', 'sc_ws', 'sc_wv', 'lin2_ws', 'lin2_wv')}
    del _L1_gnn_all

    def _L2_gnn_setup():
        import jax, jax.numpy as jnp
        import numpy as np
        MUL0, MUL1 = (64, 32)
        INV_SQRT3 = 1.0 / np.sqrt(3.0)

        def _split(x):
            return (x[:, :MUL0], x[:, MUL0:].reshape(x.shape[0], MUL1, 3))

        def _merge(o0, o1):
            return jnp.concatenate([o0, o1.reshape(o1.shape[0], -1)], axis=-1)

        def _tp(x0, x1, y0, y1, w000, w011, w101, w110):
            fan0 = x0.shape[1] * y0.shape[1] + x1.shape[1] * y1.shape[1]
            fan1 = x0.shape[1] * y1.shape[1] + x1.shape[1] * y0.shape[1]
            out0 = (jnp.einsum('eu,ev,uvw->ew', x0, y0, w000) + INV_SQRT3 * jnp.einsum('euk,evk,uvw->ew', x1, y1, w110)) / np.sqrt(fan0)
            out1 = (jnp.einsum('eu,evk,uvw->ewk', x0, y1, w011) + jnp.einsum('euk,ev,uvw->ewk', x1, y0, w101)) / np.sqrt(fan1)
            return (out0, out1)

        def _lin(x0, x1, w0, w1):
            return (x0 @ w0 / np.sqrt(x0.shape[1]), jnp.einsum('euk,uv->evk', x1, w1) / np.sqrt(x1.shape[1]))
        key = jax.random.key(seed)
        ks = jax.random.split(key, 20)
        N, E = (50000, 15625)
        inp = {'node_features': jax.random.normal(ks[0], (N, MUL0 + 3 * MUL1), dtype=jnp.float32), 'edge_index': jax.random.randint(ks[1], (2, E), 0, N, dtype=jnp.int64), 'edge_attr_tensor': jax.random.normal(ks[2], (E, 4), dtype=jnp.float32), 'node_attr_scalar_raw': jax.random.normal(ks[3], (N, 1), dtype=jnp.float32), 'wm000': jax.random.normal(ks[4], (MUL0, 1, MUL0), dtype=jnp.float32), 'wm011': jax.random.normal(ks[5], (MUL0, 1, MUL1), dtype=jnp.float32), 'wm101': jax.random.normal(ks[6], (MUL1, 1, MUL1), dtype=jnp.float32), 'wm110': jax.random.normal(ks[7], (MUL1, 1, MUL0), dtype=jnp.float32), 'lm0': jax.random.normal(ks[8], (MUL0, MUL0), dtype=jnp.float32), 'lm1': jax.random.normal(ks[9], (MUL1, MUL1), dtype=jnp.float32), 'wu000': jax.random.normal(ks[10], (MUL0, MUL0, MUL0), dtype=jnp.float32), 'wu011': jax.random.normal(ks[11], (MUL0, MUL1, MUL1), dtype=jnp.float32), 'wu101': jax.random.normal(ks[12], (MUL1, MUL0, MUL1), dtype=jnp.float32), 'wu110': jax.random.normal(ks[13], (MUL1, MUL1, MUL0), dtype=jnp.float32), 'lu0': jax.random.normal(ks[14], (MUL0, MUL0), dtype=jnp.float32), 'lu1': jax.random.normal(ks[15], (MUL1, MUL1), dtype=jnp.float32)}
        return inp
    _L2_gnn_all = _L2_gnn_setup()
    _L2_gnn_in = {k: v for k, v in _L2_gnn_all.items() if k in ('wm000', 'wm011', 'wm101', 'wm110', 'lm0', 'lm1', 'wu000', 'wu011', 'wu101', 'wu110', 'lu0', 'lu1')}
    del _L2_gnn_all

    def _L3_gnn_setup():
        import jax, jax.numpy as jnp
        import numpy as np
        N, E = (50000, 25000)
        MUL0, MUL1 = (64, 32)
        D = MUL0 + 3 * MUL1
        INV3 = float(1.0 / np.sqrt(3.0))
        INV6 = float(1.0 / np.sqrt(6.0))
        C0 = float(1.0 / np.sqrt(MUL0 + MUL1))
        C1 = float(np.sqrt(3.0 / (MUL0 + 2 * MUL1)))
        LIN_S = float(1.0 / np.sqrt(MUL0))
        LIN_V = float(1.0 / np.sqrt(MUL1))
        key = jax.random.key(seed)
        ks = jax.random.split(key, 10)
        x = jax.random.normal(ks[0], (N, D), dtype=jnp.float32)
        sh = jax.random.normal(ks[1], (E, 4), dtype=jnp.float32)
        edge_index = jax.random.randint(ks[2], (2, E), 0, N, dtype=jnp.int64)
        W1 = jax.random.normal(ks[3], (MUL0, MUL0), dtype=jnp.float32)
        W2 = jax.random.normal(ks[4], (MUL1, MUL0), dtype=jnp.float32)
        W3 = jax.random.normal(ks[5], (MUL0, MUL1), dtype=jnp.float32)
        W4 = jax.random.normal(ks[6], (MUL1, MUL1), dtype=jnp.float32)
        W5 = jax.random.normal(ks[7], (MUL1, MUL1), dtype=jnp.float32)
        Ws = jax.random.normal(ks[8], (MUL0, MUL0), dtype=jnp.float32)
        Wv = jax.random.normal(ks[9], (MUL1, MUL1), dtype=jnp.float32)
        return {'x': x, 'sh': sh, 'W1': W1, 'W2': W2, 'W3': W3, 'W4': W4, 'W5': W5, 'Ws': Ws, 'Wv': Wv, 'edge_index': edge_index}
    _L3_gnn_all = _L3_gnn_setup()
    _L3_gnn_in = {k: v for k, v in _L3_gnn_all.items() if k in ('W1', 'W2', 'W3', 'W4', 'W5', 'Ws', 'Wv')}
    del _L3_gnn_all
    return {'x': x, 'src': src, 'dst': dst, 'edge_attr_4': edge_attr_4, 'edge_attr_64': edge_attr_64, 'node_vec1': node_vec1, 'L0_gnn_Wm_ss': _L0_gnn_in['Wm_ss'], 'L0_gnn_Wm_vv': _L0_gnn_in['Wm_vv'], 'L0_gnn_Wm_sv': _L0_gnn_in['Wm_sv'], 'L0_gnn_Wm_vs': _L0_gnn_in['Wm_vs'], 'L0_gnn_Lm_s': _L0_gnn_in['Lm_s'], 'L0_gnn_Lm_v': _L0_gnn_in['Lm_v'], 'L0_gnn_Wu_ss': _L0_gnn_in['Wu_ss'], 'L0_gnn_Wu_vv': _L0_gnn_in['Wu_vv'], 'L0_gnn_Wu_sv': _L0_gnn_in['Wu_sv'], 'L0_gnn_Wu_vs': _L0_gnn_in['Wu_vs'], 'L0_gnn_Lu_s': _L0_gnn_in['Lu_s'], 'L0_gnn_Lu_v': _L0_gnn_in['Lu_v'], 'L1_gnn_lin1_ws': _L1_gnn_in['lin1_ws'], 'L1_gnn_lin1_wv': _L1_gnn_in['lin1_wv'], 'L1_gnn_fc_w1': _L1_gnn_in['fc_w1'], 'L1_gnn_fc_w2': _L1_gnn_in['fc_w2'], 'L1_gnn_sc_ws': _L1_gnn_in['sc_ws'], 'L1_gnn_sc_wv': _L1_gnn_in['sc_wv'], 'L1_gnn_lin2_ws': _L1_gnn_in['lin2_ws'], 'L1_gnn_lin2_wv': _L1_gnn_in['lin2_wv'], 'L2_gnn_wm000': _L2_gnn_in['wm000'], 'L2_gnn_wm011': _L2_gnn_in['wm011'], 'L2_gnn_wm101': _L2_gnn_in['wm101'], 'L2_gnn_wm110': _L2_gnn_in['wm110'], 'L2_gnn_lm0': _L2_gnn_in['lm0'], 'L2_gnn_lm1': _L2_gnn_in['lm1'], 'L2_gnn_wu000': _L2_gnn_in['wu000'], 'L2_gnn_wu011': _L2_gnn_in['wu011'], 'L2_gnn_wu101': _L2_gnn_in['wu101'], 'L2_gnn_wu110': _L2_gnn_in['wu110'], 'L2_gnn_lu0': _L2_gnn_in['lu0'], 'L2_gnn_lu1': _L2_gnn_in['lu1'], 'L3_gnn_W1': _L3_gnn_in['W1'], 'L3_gnn_W2': _L3_gnn_in['W2'], 'L3_gnn_W3': _L3_gnn_in['W3'], 'L3_gnn_W4': _L3_gnn_in['W4'], 'L3_gnn_W5': _L3_gnn_in['W5'], 'L3_gnn_Ws': _L3_gnn_in['Ws'], 'L3_gnn_Wv': _L3_gnn_in['Wv']}

def reference(x, src, dst, edge_attr_4, edge_attr_64, node_vec1, L0_gnn_Wm_ss, L0_gnn_Wm_vv, L0_gnn_Wm_sv, L0_gnn_Wm_vs, L0_gnn_Lm_s, L0_gnn_Lm_v, L0_gnn_Wu_ss, L0_gnn_Wu_vv, L0_gnn_Wu_sv, L0_gnn_Wu_vs, L0_gnn_Lu_s, L0_gnn_Lu_v, L1_gnn_lin1_ws, L1_gnn_lin1_wv, L1_gnn_fc_w1, L1_gnn_fc_w2, L1_gnn_sc_ws, L1_gnn_sc_wv, L1_gnn_lin2_ws, L1_gnn_lin2_wv, L2_gnn_wm000, L2_gnn_wm011, L2_gnn_wm101, L2_gnn_wm110, L2_gnn_lm0, L2_gnn_lm1, L2_gnn_wu000, L2_gnn_wu011, L2_gnn_wu101, L2_gnn_wu110, L2_gnn_lu0, L2_gnn_lu1, L3_gnn_W1, L3_gnn_W2, L3_gnn_W3, L3_gnn_W4, L3_gnn_W5, L3_gnn_Ws, L3_gnn_Wv):
    import jax
    import jax.numpy as jnp

    def _L0_gnn_ref(node_features, edge_index, edge_attr_tensor, node_attr_scalar_raw, Wm_ss, Wm_vv, Wm_sv, Wm_vs, Lm_s, Lm_v, Wu_ss, Wu_vv, Wu_sv, Wu_vs, Lu_s, Lu_v):
        import jax, jax.numpy as jnp
        import numpy as np
        N = 625
        E = 20000
        INV_SQRT3 = 0.5773502691896258
        INV8 = 0.125
        INV_SQRT32 = 0.17677669529663687
        INV64 = 0.015625
        INV32 = 0.03125
        INV_SQRT2048 = 0.022097086912079608
        n = node_features.shape[0]
        e = edge_attr_tensor.shape[0]
        row, col = (edge_index[0], edge_index[1])
        r_vec = edge_attr_tensor[:, :3]
        dist = edge_attr_tensor[:, 3:4]
        xj = node_features[col]
        s = xj[:, :64]
        v = xj[:, 64:].reshape(e, 32, 3)
        m0 = s @ Wm_ss * dist * INV8 + jnp.einsum('eui,ei->eu', v, r_vec) @ Wm_vv * (INV_SQRT3 * INV_SQRT32)
        m1 = (s @ Wm_sv)[:, :, None] * r_vec[:, None, :] * INV8 + jnp.einsum('eui,uw->ewi', v, Wm_vs) * dist[:, :, None] * INV_SQRT32
        m0 = m0 + s @ Lm_s * INV8
        m1 = m1 + jnp.einsum('eui,uw->ewi', v, Lm_v) * INV_SQRT32
        msg = jnp.concatenate([m0, m1.reshape(e, 96)], axis=-1)
        agg = jax.ops.segment_sum(msg, row, num_segments=n)
        a0 = agg[:, :64]
        a1 = agg[:, 64:].reshape(n, 32, 3)
        xs = node_features[:, :64]
        xv = node_features[:, 64:].reshape(n, 32, 3)
        u0 = jnp.einsum('nu,nv,uvw->nw', xs, a0, Wu_ss) * INV64 + jnp.einsum('nui,nvi,uvw->nw', xv, a1, Wu_vv) * (INV_SQRT3 * INV32)
        u1 = jnp.einsum('nu,nvi,uvw->nwi', xs, a1, Wu_sv) * INV_SQRT2048 + jnp.einsum('nui,nv,uvw->nwi', xv, a0, Wu_vs) * INV_SQRT2048
        u0 = u0 + xs @ Lu_s * INV8
        u1 = u1 + jnp.einsum('nui,uw->nwi', xv, Lu_v) * INV_SQRT32
        upd = jnp.concatenate([u0, u1.reshape(n, 96)], axis=-1)
        return node_features + upd

    def _L1_gnn_ref(node_features, node_attr, edge_src, edge_dst, edge_attr, edge_scalars, lin1_ws, lin1_wv, fc_w1, fc_w2, sc_ws, sc_wv, lin2_ws, lin2_wv):
        import jax, jax.numpy as jnp
        import numpy as np
        N, E = (1250, 20000)
        S_IN, V_IN = (64, 32)
        S_MID, V_MID = (96, 128)
        S_OUT, V_OUT = (96, 32)
        R = 64
        FC_HID = 64
        W_NUMEL = 64 + 64 + 32 + 32 + 32
        NUM_NEIGHBORS = 16.0

        def _inv(d):
            return 1.0 / jnp.sqrt(jnp.float32(d))

        def _forward(node_features, node_attr, edge_attr, edge_scalars, lin1_ws, lin1_wv, fc_w1, fc_w2, sc_ws, sc_wv, lin2_ws, lin2_wv, edge_src, edge_dst):
            n = node_features.shape[0]
            s = node_features[:, :S_IN]
            v = node_features[:, S_IN:].reshape(n, V_IN, 3)
            a = node_attr
            sc_s = s @ sc_ws * a * _inv(S_IN)
            sc_v = jnp.einsum('nci,cd->ndi', v, sc_wv) * a[:, :, None] * _inv(V_IN)
            h_s = s @ lin1_ws * a * _inv(S_IN)
            h_v = jnp.einsum('nci,cd->ndi', v, lin1_wv) * a[:, :, None] * _inv(V_IN)
            hid = jax.nn.silu(edge_scalars @ fc_w1 * _inv(R))
            w = hid @ fc_w2 * _inv(FC_HID)
            w1, w2, w3, w4, w5 = jnp.split(w, [64, 128, 160, 192], axis=-1)
            es = h_s[edge_src]
            ev = h_v[edge_src]
            e0 = edge_attr[:, :1]
            e1 = edge_attr[:, 1:4]
            m_s1 = w1 * es * e0
            m_s2 = w4 * jnp.einsum('eci,ei->ec', ev, e1) * _inv(3)
            m_v1 = (w2 * es)[:, :, None] * e1[:, None, :]
            m_v2 = w3[:, :, None] * ev * e0[:, :, None]
            m_v3 = w5[:, :, None] * jnp.cross(ev, e1[:, None, :]) * _inv(2)
            mid_s = jnp.concatenate([m_s1, m_s2], axis=-1)
            mid_v = jnp.concatenate([m_v1, m_v2, m_v3], axis=1)
            inv_nn = 1.0 / jnp.sqrt(jnp.float32(NUM_NEIGHBORS))
            agg_s = jax.ops.segment_sum(mid_s, edge_dst, num_segments=n) * inv_nn
            agg_v = jax.ops.segment_sum(mid_v, edge_dst, num_segments=n) * inv_nn
            o_s = agg_s @ lin2_ws * a * _inv(S_MID)
            o_v = jnp.einsum('nci,cd->ndi', agg_v, lin2_wv) * a[:, :, None] * _inv(V_MID)
            pre_s = sc_s + o_s
            pre_v = sc_v + o_v
            scalars = jax.nn.silu(pre_s[:, :64])
            gates = jax.nn.sigmoid(pre_s[:, 64:96])
            gated = gates[:, :, None] * pre_v
            return jnp.concatenate([scalars, gated.reshape(n, 3 * V_OUT)], axis=-1)
        return _forward(node_features, node_attr, edge_attr, edge_scalars, lin1_ws, lin1_wv, fc_w1, fc_w2, sc_ws, sc_wv, lin2_ws, lin2_wv, edge_src, edge_dst)

    def _L2_gnn_ref(node_features, edge_index, edge_attr_tensor, node_attr_scalar_raw, wm000, wm011, wm101, wm110, lm0, lm1, wu000, wu011, wu101, wu110, lu0, lu1):
        import jax, jax.numpy as jnp
        import numpy as np
        MUL0, MUL1 = (64, 32)
        INV_SQRT3 = 1.0 / np.sqrt(3.0)

        def _split(x):
            return (x[:, :MUL0], x[:, MUL0:].reshape(x.shape[0], MUL1, 3))

        def _merge(o0, o1):
            return jnp.concatenate([o0, o1.reshape(o1.shape[0], -1)], axis=-1)

        def _tp(x0, x1, y0, y1, w000, w011, w101, w110):
            fan0 = x0.shape[1] * y0.shape[1] + x1.shape[1] * y1.shape[1]
            fan1 = x0.shape[1] * y1.shape[1] + x1.shape[1] * y0.shape[1]
            out0 = (jnp.einsum('eu,ev,uvw->ew', x0, y0, w000) + INV_SQRT3 * jnp.einsum('euk,evk,uvw->ew', x1, y1, w110)) / np.sqrt(fan0)
            out1 = (jnp.einsum('eu,evk,uvw->ewk', x0, y1, w011) + jnp.einsum('euk,ev,uvw->ewk', x1, y0, w101)) / np.sqrt(fan1)
            return (out0, out1)

        def _lin(x0, x1, w0, w1):
            return (x0 @ w0 / np.sqrt(x0.shape[1]), jnp.einsum('euk,uv->evk', x1, w1) / np.sqrt(x1.shape[1]))
        N = node_features.shape[0]
        row, col = (edge_index[0], edge_index[1])
        r_vec = edge_attr_tensor[:, :3]
        dist = edge_attr_tensor[:, 3:4]
        e0 = dist
        e1 = r_vec[:, None, :]
        xj0, xj1 = _split(node_features[col])
        m0, m1 = _tp(xj0, xj1, e0, e1, wm000, wm011, wm101, wm110)
        d0, d1 = _lin(xj0, xj1, lm0, lm1)
        msgs = _merge(m0 + d0, m1 + d1)
        agg = jax.ops.segment_sum(msgs, row, num_segments=N)
        a0, a1 = _split(agg)
        x0, x1 = _split(node_features)
        u0, u1 = _tp(x0, x1, a0, a1, wu000, wu011, wu101, wu110)
        ud0, ud1 = _lin(x0, x1, lu0, lu1)
        return node_features + _merge(u0 + ud0, u1 + ud1)

    def _L3_gnn_ref(x, sh, W1, W2, W3, W4, W5, Ws, Wv, edge_index):
        import jax, jax.numpy as jnp
        import numpy as np
        N, E = (50000, 25000)
        MUL0, MUL1 = (64, 32)
        D = MUL0 + 3 * MUL1
        INV3 = float(1.0 / np.sqrt(3.0))
        INV6 = float(1.0 / np.sqrt(6.0))
        C0 = float(1.0 / np.sqrt(MUL0 + MUL1))
        C1 = float(np.sqrt(3.0 / (MUL0 + 2 * MUL1)))
        LIN_S = float(1.0 / np.sqrt(MUL0))
        LIN_V = float(1.0 / np.sqrt(MUL1))
        n = x.shape[0]
        src, dst = (edge_index[0], edge_index[1])
        s = x[:, :MUL0]
        v = x[:, MUL0:].reshape(n, MUL1, 3)
        ss, vv = (s[src], v[src])
        e0 = sh[:, 0:1]
        e1 = sh[:, 1:4]
        dot = jnp.einsum('eui,ei->eu', vv, e1)
        out0 = C0 * (ss * e0 @ W1 + dot * INV3 @ W2)
        p3 = (ss @ W3)[:, :, None] * e1[:, None, :] * INV3
        p4 = jnp.einsum('eui,uw->ewi', vv * e0[:, :, None], W4) * INV3
        p5 = jnp.einsum('eui,uw->ewi', jnp.cross(vv, e1[:, None, :]), W5) * INV6
        out1 = C1 * (p3 + p4 + p5)
        m = jnp.concatenate([out0, out1.reshape(-1, 3 * MUL1)], axis=1)
        m_agg = jax.ops.segment_sum(m, dst, num_segments=n)
        hs = m_agg[:, :MUL0] @ Ws * LIN_S
        hv = jnp.einsum('nui,uw->nwi', m_agg[:, MUL0:].reshape(n, MUL1, 3), Wv) * LIN_V
        h = jnp.concatenate([hs, hv.reshape(n, 3 * MUL1)], axis=1)
        return x + jax.nn.relu(h)
    edge_index = jnp.stack([src, dst])
    h = jnp.maximum(_layernorm(x, axis=-1), 0.0)
    x = x + _L0_gnn_ref(h, edge_index, edge_attr_4, node_vec1, L0_gnn_Wm_ss, L0_gnn_Wm_vv, L0_gnn_Wm_sv, L0_gnn_Wm_vs, L0_gnn_Lm_s, L0_gnn_Lm_v, L0_gnn_Wu_ss, L0_gnn_Wu_vv, L0_gnn_Wu_sv, L0_gnn_Wu_vs, L0_gnn_Lu_s, L0_gnn_Lu_v)
    h = jnp.maximum(_layernorm(x, axis=-1), 0.0)
    x = x + _L1_gnn_ref(h, node_vec1, src, dst, edge_attr_4, edge_attr_64, L1_gnn_lin1_ws, L1_gnn_lin1_wv, L1_gnn_fc_w1, L1_gnn_fc_w2, L1_gnn_sc_ws, L1_gnn_sc_wv, L1_gnn_lin2_ws, L1_gnn_lin2_wv)
    h = jnp.maximum(_layernorm(x, axis=-1), 0.0)
    x = x + _L2_gnn_ref(h, edge_index, edge_attr_4, node_vec1, L2_gnn_wm000, L2_gnn_wm011, L2_gnn_wm101, L2_gnn_wm110, L2_gnn_lm0, L2_gnn_lm1, L2_gnn_wu000, L2_gnn_wu011, L2_gnn_wu101, L2_gnn_wu110, L2_gnn_lu0, L2_gnn_lu1)
    h = jnp.maximum(_layernorm(x, axis=-1), 0.0)
    x = x + _L3_gnn_ref(h, edge_attr_4, L3_gnn_W1, L3_gnn_W2, L3_gnn_W3, L3_gnn_W4, L3_gnn_W5, L3_gnn_Ws, L3_gnn_Wv, edge_index)
    return x

_drawn_inputs = setup_inputs


def setup_inputs(seed=0):
    import zlib

    import numpy as np

    out = dict(_drawn_inputs(seed))
    spreads = {}
    factors = {'L1_gnn_lin1_ws': 2.783,
     'L1_gnn_lin1_wv': 3.71,
     'L1_gnn_sc_wv': 3.495,
     'L1_gnn_lin2_ws': 3.021,
     'L1_gnn_lin2_wv': 3.533}
    for name, (base, spread) in spreads.items():
        noise = np.random.default_rng([zlib.crc32(name.encode()), seed]).standard_normal(out[name].shape)
        drawn = base * np.exp(spread * noise) if base else spread * noise
        out[name] = jnp.asarray(drawn.astype(out[name].dtype))
    for name, factor in factors.items():
        out[name] = (out[name] * factor).astype(out[name].dtype)
    return out
```

```python
from contextlib import ExitStack
from math import sqrt

import concourse.bass as bass
from concourse import mybir

ALU = mybir.AluOpType
ACT = mybir.ActivationFunctionType
AX_X = mybir.AxisListType.X
F32 = mybir.dt.float32
I32 = mybir.dt.int32
U32 = mybir.dt.uint32

P = 128
N = 3125
E = 100000
S, V, C3 = 64, 32, 3
F = S + C3 * V
BLOCKS = -(-N // P)
NODES = BLOCKS * P
COLS = -(-E // P)
PADS = COLS * P - E
PAIR = 2 * P
GROUP = 4
SLOTS = 4
PAIRS = -(-(E // PAIR + BLOCKS) // (GROUP * SLOTS // 2)) * (GROUP * SLOTS // 2)
TILES = 2 * PAIRS
GROUPS = TILES // GROUP
TURNS = GROUPS // SLOTS
ROW = TILES + 1
BUCKETS = BLOCKS + 1
REC_S = 6
REC_D = 70
R_ = 64
CHUNK = 17
CHUNKS = COLS // CHUNK
FILL = 49
W_MSG = 4 * P + V
W_TP = 3 * P + S + V
KINDS = 5
PART = W_MSG * BLOCKS
BANK = 512
ISQ3 = 0.5773502691896258
assert CHUNKS * CHUNK == COLS and CHUNKS % 2 == 0 and ROW % FILL == 0 and PADS <= P
assert GROUPS % SLOTS == 0


def program(nc, a, out):
    with ExitStack() as ctx:
        def sb(name, cols, dt=F32, rows=P):
            return ctx.enter_context(nc.sbuf_tensor(name, [rows, cols], dt))

        def sem(name):
            return ctx.enter_context(nc.semaphore(name))

        slots_src = nc.dram_tensor("slots_src", (P * ROW, REC_S), F32, kind="Internal").ap()
        slots_dst = nc.dram_tensor("slots_dst", (P * ROW, REC_D), F32, kind="Internal").ap()
        table = [nc.dram_tensor(f"table{n}", (NODES, F), F32, kind="Internal").ap() for n in range(4)]

        x = sb("x", BLOCKS * F)
        h = sb("h", BLOCKS * F)
        sums = sb("sums", PART)
        scale_a = sb("scale_a", BLOCKS)
        w_outer = sb("w_outer", 40 * S)
        w_sv = sb("w_sv", V * V)
        w_vs = sb("w_vs", V * V)
        iota_row = sb("iota_row", P)
        ident = sb("ident", P)
        before = sb("before", P)
        ones = sb("ones", P)
        offs_src = sb("offs_src", PAIRS, I32, 1)
        offs_dst = sb("offs_dst", PAIRS, I32, 1)

        r96, r32, r128 = 1 / sqrt(96), 1 / sqrt(32), 1 / sqrt(128)
        c0, c1, c6 = 1 / sqrt(S + V), sqrt(3.0 / (S + 2 * V)), 1 / sqrt(6.0)
        w2 = a["L1_gnn_fc_w2"]
        plan = [
            ("s0", S, [(0, S, a["L0_gnn_Wm_ss"], .125), (S, S, a["L0_gnn_Lm_s"], .125)]),
            ("d0", S, [(0, V, a["L0_gnn_Wm_vv"], ISQ3 * r32)]),
            ("v0", V, [(0, S, a["L0_gnn_Wm_sv"], .125), (S, V, a["L0_gnn_Wm_vs"], r32), (96, V, a["L0_gnn_Lm_v"], r32)]),
            ("us0", S, [(0, S, a["L0_gnn_Lu_s"], .125)]),
            ("uv0", V, [(0, V, a["L0_gnn_Lu_v"], r32)]),
            ("s2", S, [(0, S, a["L2_gnn_wm000"], r96), (S, S, a["L2_gnn_lm0"], .125)]),
            ("d2", S, [(0, V, a["L2_gnn_wm110"], ISQ3 * r96)]),
            ("v2", V, [(0, S, a["L2_gnn_wm011"], r96), (S, V, a["L2_gnn_wm101"], r96), (96, V, a["L2_gnn_lm1"], r32)]),
            ("us2", S, [(0, S, a["L2_gnn_lu0"], .125)]),
            ("uv2", V, [(0, V, a["L2_gnn_lu1"], r32)]),
            ("lin_s", S, [(0, S, a["L1_gnn_lin1_ws"], .125)]),
            ("lin_v", V, [(0, V, a["L1_gnn_lin1_wv"], r32)]),
            ("fc1", R_, [(0, R_, a["L1_gnn_fc_w1"], 1.0)]),
            ("fc_a", 160, [(0, R_, w2[:, 0:160], .125)]),
            ("fc_b", V, [(0, R_, w2[:, 192:224], .125)]),
            ("fc_c", V, [(0, R_, w2[:, 192:224], -.125)]),
            ("fc_d", V, [(0, R_, w2[:, 160:192], .125)]),
            ("out_s", 96, [(0, S, a["L1_gnn_lin2_ws"][0:S, :], .25 * r96), (S, V, a["L1_gnn_lin2_ws"][S:96, :], .25 * r96 / sqrt(3))]),
            ("out_v", V, [(0, 96, a["L1_gnn_lin2_wv"][0:96, :], .25 * r128), (96, V, a["L1_gnn_lin2_wv"][96:P, :], .25 * r128 / sqrt(2))]),
            ("sc_s", 96, [(0, S, a["L1_gnn_sc_ws"], .125)]),
            ("sc_v", V, [(0, V, a["L1_gnn_sc_wv"], r32)]),
            ("m_s", S, [(0, S, a["L3_gnn_W1"], c0), (S, V, a["L3_gnn_W2"], c0 * ISQ3)]),
            ("m_v", V, [(0, S, a["L3_gnn_W3"], c1 * ISQ3), (S, V, a["L3_gnn_W4"], c1 * ISQ3), (96, V, a["L3_gnn_W5"], c1 * c6)]),
            ("h_s", S, [(0, S, a["L3_gnn_Ws"], .125)]),
            ("h_v", V, [(0, V, a["L3_gnn_Wv"], r32)]),
        ]
        small = sb("small", sum(c for _, c, _ in plan))
        w, at = {}, 0
        for name, cols, parts in plan:
            rows = max(r + n for r, n, _, _ in parts)
            w[name] = (at, rows, cols)
            at += cols

        def wt(name, cols=None):
            c, rows, n = w[name]
            return small[0:rows, c:c + (cols or n)]

        loads = [(small[r:r + n, w[name][0]:w[name][0] + cols], src, k)
                 for name, cols, parts in plan for r, n, src, k in parts]

        shared = sb("shared", 16064)

        def repeat(ap, dim, n):
            shape = list(ap.shape)
            shape[dim] = n
            return ap.broadcast_to(shape)

        class Area:
            def __init__(self, tensor):
                self.t, self.at = tensor, 0

            def take(self, cols, rows=P):
                v = self.t[0:rows, self.at:self.at + cols]
                self.at += cols
                assert self.at <= self.t.shape[1]
                return v

        area = Area(shared)
        rec_s = area.take(SLOTS * GROUP * REC_S).rearrange("p (s t r) -> p s t r", s=SLOTS, t=GROUP)
        rec_d = area.take(SLOTS * GROUP * REC_D).rearrange("p (s t r) -> p s t r", s=SLOTS, t=GROUP)
        rows_x = area.take(SLOTS * GROUP * F).rearrange("p (s t f) -> p s t f", s=SLOTS, t=GROUP)
        hot = area.take(2 * GROUP * KINDS * P).rearrange("p (s t k n) -> p s t k n", s=2, t=GROUP, k=KINDS)
        msg = area.take(2 * GROUP * 512).rearrange("p (s t f) -> p s t f", s=2, t=GROUP)
        neg = area.take(2 * GROUP * 96).rearrange("p (s t f) -> p s t f", s=2, t=GROUP)
        es_t = area.take(BANK, R_)
        hid = area.take(BANK, R_)
        area = Area(shared)
        st_g = area.take(W_MSG)
        st_h = area.take(F)
        st_a = area.take(1)
        g_t = area.take(4 * P)
        d_t = area.take(P, V)
        s_t = area.take(P, S)
        v_t = area.take(3 * P, V)
        agg = area.take(F)
        agg_t = area.take(4 * P)
        outer = area.take(40 * P)
        outer_tmp = area.take(V * V)
        outer_t = area.take(2 * BANK).rearrange("p (s n) -> p s n", s=2)
        prod = area.take(2 * 3 * V * V).rearrange("p (k n) -> p k n", k=2)
        fin = area.take(192)
        area = Area(sums)
        square = area.take(BLOCKS * F)
        proj = area.take(BLOCKS * F)
        mean = sb("mean", BLOCKS)
        var = sb("var", BLOCKS)
        area = Area(sums)
        key = [area.take(COLS).bitcast(I32) for _ in range(2)]
        loc = [area.take(COLS) for _ in range(2)]
        addr = [area.take(COLS).bitcast(I32) for _ in range(2)]
        stage_s = area.take(2 * CHUNK * REC_S).rearrange("p (s c r) -> p s c r", s=2, c=CHUNK)
        stage_d = area.take(2 * CHUNK * REC_D).rearrange("p (s c r) -> p s c r", s=2, c=CHUNK)
        to_s = area.take(2 * CHUNK).bitcast(U32).rearrange("p (s c) -> p s c", s=2)
        to_d = area.take(2 * CHUNK).bitcast(U32).rearrange("p (s c) -> p s c", s=2)
        blk = area.take(COLS)
        is_b = area.take(COLS)
        upto = area.take(COLS)
        rank = area.take(COLS)
        zero = area.take(COLS)
        area = Area(shared)
        fill = area.take(FILL * REC_D)
        fill_s = area.take(FILL * REC_S)
        temp_i = area.take(COLS).bitcast(I32)
        temp_j = area.take(COLS).bitcast(I32)
        bucket_no = area.take(BUCKETS)
        count = area.take(BUCKETS)
        total_i = area.take(BUCKETS).bitcast(I32)
        supers = area.take(BUCKETS)
        ends = area.take(BUCKETS)
        start = area.take(BUCKETS)
        iota_pairs = area.take(PAIRS, 1)
        block_of = area.take(PAIRS, 1)

        psum = ctx.enter_context(nc.psum_tensor("psum", [P, 8 * BANK], F32))

        def bank(n, lo=0, hi=BANK, rows=P):
            return psum[0:rows, n * BANK + lo:n * BANK + hi]

        consts_ready = sem("consts_ready")
        loaded = sem("loaded")
        weights_loaded = sem("weights_loaded")
        outer_loaded = [sem("outer_loaded0"), sem("outer_loaded2")]
        filled_dram = sem("filled_dram")
        fill_ready = sem("fill_ready")
        v_step = sem("v_step")
        counted = sem("counted")
        prefixed = sem("prefixed")
        chunk_loaded = [sem(f"chunk_loaded{s}") for s in range(2)]
        chunk_filled = [sem(f"chunk_filled{s}") for s in range(2)]
        chunk_scattered = [sem(f"chunk_scattered{s}") for s in range(2)]
        phase = sem("phase")
        centred = sem("centred")
        squared = sem("squared")
        var_ready = sem("var_ready")
        root_ready = sem("root_ready")
        normed = sem("normed")
        table_written = sem("table_written")
        rec_ready = [sem(f"rec_ready{s}") for s in range(SLOTS)]
        x_ready = [sem(f"x_ready{s}") for s in range(SLOTS)]
        hot_ready = sem("hot_ready")
        neg_ready = sem("neg_ready")
        scattered = sem("scattered")
        added = sem("added")
        es_turned = sem("es_turned")
        es_copied = sem("es_copied")
        hid_ready = sem("hid_ready")
        hid_copied = sem("hid_copied")
        w_ready = sem("w_ready")
        msg_ready = sem("msg_ready")
        n_staged = sem("n_staged")
        n_turned = sem("n_turned")
        n_copied = sem("n_copied")
        n_mixed = sem("n_mixed")
        n_mixed_copied = sem("n_mixed_copied")
        n_partial = sem("n_partial")
        n_prod = sem("n_prod")
        n_outer_ss = sem("n_outer_ss")
        n_outer_vv = sem("n_outer_vv")
        n_z_turned = sem("n_z_turned")
        n_z_copied = sem("n_z_copied")
        n_summed = sem("n_summed")
        n_gated = sem("n_gated")
        n_done = sem("n_done")
        stored = sem("stored")

        block = ctx.enter_context(nc.Block())

        class Steps:

            def __init__(self, eng, s):
                self.eng, self.sem, self.n = eng, s, 0

            def __call__(self, ins):
                ins.then_inc(self.sem, 1)
                self.n += 1
                self.eng.wait_ge(self.sem, self.n)

            def at(self, ins, i, k, per):
                ins.then_inc(self.sem, 1)
                self.eng.wait_ge(self.sem, i * per + (self.n + k))

        def meet(eng, k):
            eng.drain().then_inc(phase, 1)
            eng.wait_ge(phase, 5 * k)

        BLOCKS_BEFORE = [0, BLOCKS, 2 * BLOCKS, 3 * BLOCKS]
        NODE_TURNS = [0, 2 * BLOCKS, 3 * BLOCKS, 4 * BLOCKS]
        LAYER_WIDTH = [W_MSG, W_TP, W_MSG, W_TP]
        K_NORM, K_EDGE, K_NODE = range(3)

        def phase_no(layer, k):
            return 3 + 3 * layer + k

        def turns(eng, n, body):
            body(0, True)
            with eng.Fori(1, n) as i:
                body(i, False)

        def parts(layer, slot, t):
            if layer == 1:
                m = msg[:, slot % 2, t, :]
                return (m[:, 0:64], m[:, 128:224], m[:, 64:128], m[:, 224:320], m[:, 320:416], m[:, 416:512])
            r = rows_x[:, slot, t, :]
            v = r[:, S:F]
            return (r[:, 0:S], v, r[:, 0:S], v, neg[:, slot % 2, t, :], v)

        @block.sync
        def _(sp):
            sp.dma_start(x[:, :].rearrange("p (b f) -> p b f", f=F),
                         a["x"].rearrange("(b p) f -> p b f", p=P)).then_inc(loaded, 16)
            sp.dma_start(key[0], a["src"]).then_inc(loaded, 16)
            sp.dma_start(key[1], a["dst"]).then_inc(loaded, 16)
            sp.dma_start(scale_a[:, :], a["node_vec1"]).then_inc(loaded, 16)
            sp.wait_ge(fill_ready, 2)
            sp.dma_start(slots_src.rearrange("(p k n) r -> p k (n r)", p=P, n=FILL),
                         repeat(fill_s.rearrange("p (o c) -> p o c", o=1), 1, ROW // FILL)).then_inc(filled_dram, 16)
            sp.dma_start(slots_dst.rearrange("(p k n) r -> p k (n r)", p=P, n=FILL),
                         repeat(fill.rearrange("p (o c) -> p o c", o=1), 1, ROW // FILL)).then_inc(filled_dram, 16)
            for dst, src, _ in loads:
                sp.dma_start(dst, src).then_inc(weights_loaded, 16)

            def load_outer(k):
                n = ("L0_gnn_Wu_ss", "L0_gnn_Wu_vv", "L0_gnn_Wu_sv", "L0_gnn_Wu_vs") if k == 0 else \
                    ("L2_gnn_wu000", "L2_gnn_wu110", "L2_gnn_wu011", "L2_gnn_wu101")
                wo = w_outer[:, :].rearrange("p (c w) -> p c w", w=S)
                sp.dma_start(wo[:, 0:32, :], a[n[0]].rearrange("(c p) w -> p c w", p=P)).then_inc(outer_loaded[k], 16)
                sp.dma_start(wo[:, 32:40, :], a[n[1]].rearrange("(c p) w -> p c w", p=P)).then_inc(outer_loaded[k], 16)
                sp.dma_start(w_sv[0:S, :], a[n[2]]).then_inc(outer_loaded[k], 16)
                sp.dma_start(w_vs[0:S, :].rearrange("v (u w) -> v u w", w=V),
                             a[n[3]].rearrange("u v w -> v u w")).then_inc(outer_loaded[k], 16)

            load_outer(0)
            sp.wait_ge(filled_dram, 32)
            meet(sp, 1)

            def chunk(i, first):
                for s in range(2):
                    if not first:
                        sp.wait_ge(chunk_scattered[s], i * (2 * CHUNK * 16))
                    sp.dma_start(stage_d[:, s, :, 2:REC_D],
                                 a["attrs"][:, bass.ds((i * 2 + s) * CHUNK, CHUNK), :]).then_inc(chunk_loaded[s], 16)

            turns(sp, CHUNKS // 2, chunk)
            for s in range(2):
                sp.wait_ge(chunk_scattered[s], CHUNKS // 2 * 2 * CHUNK * 16)
            meet(sp, 2)

            for layer in range(4):
                sp.wait_ge(phase, 5 * (phase_no(layer, K_NORM) - 1) + 4)
                rows = proj if layer == 1 else h[:, :]
                sp.dma_start(table[layer].rearrange("(b p) f -> p b f", p=P),
                             rows.rearrange("p (b f) -> p b f", f=F)).then_inc(table_written, 16)
                sp.wait_ge(table_written, 16 * (layer + 1))
                meet(sp, phase_no(layer, K_NORM))
                slots, rec, width = (slots_src, rec_s, REC_S) if layer % 2 == 0 else (slots_dst, rec_d, REC_D)
                slots = slots.rearrange("(p t) r -> p (t r)", p=P)

                def load(i, first):
                    for s in range(SLOTS):
                        if not first:
                            sp.wait_ge(scattered, i * (2 * SLOTS) + (PAIRS * layer + 2 * s + 2 - 2 * SLOTS))
                        sp.dma_start(rec[:, s, :, :].rearrange("p t r -> p (t r)"),
                                     slots[:, bass.ds((i * SLOTS + s) * (GROUP * width), GROUP * width)]).then_inc(rec_ready[s], 16)

                turns(sp, TURNS, load)
                meet(sp, phase_no(layer, K_EDGE))
                meet(sp, phase_no(layer, K_NODE))
                if layer == 0:
                    load_outer(1)
            sp.dma_start(out.rearrange("(b p) f -> p b f", p=P),
                         x[:, :].rearrange("p (b f) -> p b f", f=F)).then_inc(stored, 16)
            sp.wait_ge(stored, 16)

        @block.gpsimd
        def _(pool):
            pool.iota(iota_row[:, :], [[1, P]], base=0, channel_multiplier=0,
                      allow_small_or_imprecise_dtypes=True).then_inc(consts_ready, 1)
            pool.iota(bucket_no, [[1, BUCKETS]], base=0, channel_multiplier=0,
                      allow_small_or_imprecise_dtypes=True).then_inc(consts_ready, 1)
            pool.iota(iota_pairs, [[1, PAIRS]], base=0, channel_multiplier=0,
                      allow_small_or_imprecise_dtypes=True).then_inc(consts_ready, 1)
            pool.memset(ones[:, :], 1.0).then_inc(consts_ready, 1)
            pool.wait_ge(consts_ready, 4)
            pool.affine_select(out=ident[:, :], in_=ones[:, :], compare_op=ALU.is_equal, fill=0.0, base=0,
                               pattern=[[-1, P]], channel_multiplier=1).then_inc(consts_ready, 1)
            pool.affine_select(out=before[:, :], in_=ones[:, :], compare_op=ALU.is_gt, fill=0.0, base=0,
                               pattern=[[1, P]], channel_multiplier=-1).then_inc(consts_ready, 1)
            pool.wait_ge(consts_ready, 6)
            meet(pool, 1)

            def chunk(i, first):
                for s in range(2):
                    pool.wait_ge(chunk_filled[s], 1)
                    pool.sem_clear(chunk_filled[s])
                    for c in range(CHUNK):
                        pool.indirect_dma_start(out=slots_src, out_offset=bass.IndirectOffsetOnAxis(ap=to_s[:, s, c:c + 1], axis=0),
                                                in_=stage_s[:, s, c, :], in_offset=None).then_inc(chunk_scattered[s], 16)
                        pool.indirect_dma_start(out=slots_dst, out_offset=bass.IndirectOffsetOnAxis(ap=to_d[:, s, c:c + 1], axis=0),
                                                in_=stage_d[:, s, c, :], in_offset=None).then_inc(chunk_scattered[s], 16)

            turns(pool, CHUNKS // 2, chunk)
            meet(pool, 2)
            for layer in range(4):
                meet(pool, phase_no(layer, K_NORM))
                rec = rec_s if layer % 2 == 0 else rec_d

                def gather(i, first):
                    for s in range(SLOTS):
                        pool.wait_ge(rec_ready[s], 16)
                        pool.sem_clear(rec_ready[s])
                        for t in range(GROUP):
                            pool.indirect_dma_start(out=rows_x[:, s, t, :], out_offset=None, in_=table[layer],
                                                    in_offset=bass.IndirectOffsetOnAxis(ap=rec[:, s, t, 0:1].bitcast(U32), axis=0)
                                                    ).then_inc(x_ready[s], 16)

                turns(pool, TURNS, gather)
                meet(pool, phase_no(layer, K_EDGE))
                if layer in (0, 2):
                    base = BLOCKS * (layer // 2)

                    def outers(i, first):
                        pool.wait_ge(n_mixed_copied, i + (NODE_TURNS[layer] + 1))
                        if not first:
                            pool.wait_ge(n_z_turned, i * 10 + 10 * base)
                        pool.tensor_tensor(outer[:, 0:S * S].rearrange("p (u v) -> p u v", v=S),
                                           repeat(st_h[:, 0:S].rearrange("p (u o) -> p u o", o=1), 2, S),
                                           repeat(agg[:, 0:S].rearrange("p (o v) -> p o v", o=1), 1, S),
                                           ALU.mult).then_inc(n_outer_ss, 1)

                    turns(pool, BLOCKS, outers)
                meet(pool, phase_no(layer, K_NODE))

        @block.scalar
        def _(act):
            act.wait_ge(weights_loaded, 16 * len(loads))
            for dst, _, k in loads:
                if k != 1.0:
                    nc.scalar.mul(dst, dst, k)

            def scale_outer(k):
                act.wait_ge(outer_loaded[k], 64)
                kss, kvv, kt = (1 / 64, ISQ3 / 32, 1 / sqrt(2048) / 1.0) if k == 0 else (1 / sqrt(5120), ISQ3 / sqrt(5120), 1 / 64)
                nc.scalar.mul(w_outer[:, 0:32 * S], w_outer[:, 0:32 * S], kss)
                nc.scalar.mul(w_outer[:, 32 * S:], w_outer[:, 32 * S:], kvv)
                nc.scalar.mul(w_sv[0:S, :], w_sv[0:S, :], kt)
                nc.scalar.mul(w_vs[0:S, :], w_vs[0:S, :], kt)

            scale_outer(0)
            meet(act, 1)
            meet(act, 2)
            for layer in range(4):
                act.wait_ge(centred, layer + 1)
                nc.scalar.activation(square, h[:, :], ACT.Square).then_inc(squared, 1)
                act.wait_ge(var_ready, layer + 1)
                nc.scalar.activation(var[:, :], var[:, :], ACT.Sqrt).then_inc(root_ready, 1)
                if layer == 1:
                    def project(i, first):
                        if first:
                            act.wait_ge(normed, layer + 1)
                        else:
                            act.wait_ge(n_mixed_copied, i + BLOCKS)
                        nc.scalar.copy(st_h, h[:, bass.ds(i * F, F)])
                        nc.scalar.copy(st_a, scale_a[:, bass.ds(i, 1)]).then_inc(n_staged, 1)
                        act.wait_ge(n_turned, i + (BLOCKS + 1))
                        nc.scalar.copy(s_t, bank(0, 0, P, S))
                        nc.scalar.copy(v_t, bank(1, 0, 3 * P, V)).then_inc(n_copied, 1)
                        act.wait_ge(n_mixed, i + (BLOCKS + 1))
                        nc.scalar.activation(proj[:, bass.ds(i * F, F)], bank(2, 0, F), ACT.Copy, scale=st_a
                                             ).then_inc(n_mixed_copied, 1)

                    turns(act, BLOCKS, project)
                meet(act, phase_no(layer, K_NORM))

                if layer == 1:
                    def hidden(i, first):
                        for s in range(SLOTS):
                            act.wait_ge(es_turned, i * SLOTS + (s + 1))
                            if not (first and s == 0):
                                act.wait_ge(hid_ready, i * SLOTS + s)
                            nc.scalar.copy(es_t, bank(4, 0, BANK, R_)).then_inc(es_copied, 1)
                            act.wait_ge(hid_ready, i * SLOTS + (s + 1))
                            if not (first and s == 0):
                                act.wait_ge(w_ready, i * SLOTS + s)
                            nc.scalar.activation(hid, bank(5, 0, BANK, R_), ACT.Silu, scale=.125).then_inc(hid_copied, 1)

                    turns(act, TURNS, hidden)
                if layer == 3:
                    def negate(i, first):
                        for s in range(SLOTS):
                            act.wait_ge(x_ready[s], i * 64 + 64 * (TURNS * layer + 1))
                            if not (first and s < 2):
                                act.wait_ge(scattered, i * (2 * SLOTS) + (PAIRS * layer + 2 * s - 2))
                            nc.scalar.mul(neg[:, s % 2, :, :], rows_x[:, s, :, S:F], -1.0).then_inc(neg_ready, 1)

                    turns(act, TURNS, negate)
                meet(act, phase_no(layer, K_EDGE))

                width = LAYER_WIDTH[layer]
                nth = NODE_TURNS[layer]

                def node(i, first):
                    if not first:
                        act.wait_ge(n_done, i + BLOCKS_BEFORE[layer])
                    nc.scalar.copy(st_g[:, 0:width], sums[:, bass.ds(i * width, width)])
                    if layer == 1:
                        nc.scalar.copy(st_a, scale_a[:, bass.ds(i, 1)])
                    nc.scalar.copy(st_h, h[:, bass.ds(i * F, F)]).then_inc(n_staged, 1)
                    act.wait_ge(n_turned, i + (nth + 1))
                    nc.scalar.copy(g_t[:, :] if layer in (0, 2) else g_t[:, 0:3 * P],
                                   bank(0) if layer in (0, 2) else bank(0, 0, 3 * P))
                    if layer in (0, 2):
                        nc.scalar.copy(d_t, bank(1, 0, P, V))
                    else:
                        nc.scalar.copy(g_t[0:96, 3 * P:], bank(0, 3 * P, BANK, 96))
                    nc.scalar.copy(s_t, bank(1, P, 2 * P, S))
                    nc.scalar.copy(v_t, bank(2, 0, 3 * P, V)).then_inc(n_copied, 1)
                    act.wait_ge(n_mixed, i + (nth + 1))
                    if layer in (0, 2):
                        nc.scalar.copy(agg_t[0:S, 0:P], bank(3, F, F + P, S))
                        nc.scalar.copy(agg, bank(3, 0, F)).then_inc(n_mixed_copied, 1)
                        for c in range(10):
                            act.wait_ge(n_z_turned, i * 10 + (10 * BLOCKS * (layer // 2) + c + 1))
                            nc.scalar.copy(outer_t[:, c % 2, :], bank(c % 2)).then_inc(n_z_copied, 1)
                    if layer == 1:
                        nc.scalar.activation(fin[:, 0:192], bank(3, 0, 192), ACT.Copy, scale=st_a).then_inc(n_mixed_copied, 1)
                        act.wait_ge(n_mixed_copied, i + (nth + 1))
                        nc.scalar.activation(agg[:, 0:S], fin[:, 0:S], ACT.Silu)
                        nc.scalar.activation(st_g[:, 0:V], fin[:, S:96], ACT.Sigmoid).then_inc(n_gated, 1)
                    if layer == 3:
                        nc.scalar.copy(agg_t[0:S, 0:P], bank(3, 0, P, S))
                        nc.scalar.copy(agg_t[0:V, P:4 * P], bank(3, P, 4 * P, V)).then_inc(n_mixed_copied, 1)
                        act.wait_ge(n_summed, i + (2 * BLOCKS + 1))
                        nc.scalar.activation(fin[:, 0:F], bank(4, 0, F), ACT.Relu).then_inc(n_gated, 1)

                turns(act, BLOCKS, node)
                if layer == 0:
                    meet(act, phase_no(layer, K_NODE))
                    scale_outer(1)
                else:
                    meet(act, phase_no(layer, K_NODE))

        @block.tensor
        def _(pe):
            mm = nc.tensor.matmul
            for k in range(2):
                pe.wait_ge(counted, k + 1)
                pe.wait_ge(consts_ready, 6)
                mm(bank(0, 0, BUCKETS), before[:, :], count, start=True, stop=True)
                mm(bank(1, 0, BUCKETS), ones[:, :], count, start=True, stop=True).then_inc(prefixed, 1)
            meet(pe, 1)
            meet(pe, 2)
            for layer in range(4):
                if layer == 1:
                    def project(i, first):
                        pe.wait_ge(n_staged, i + (BLOCKS + 1))
                        for c in range(3):
                            nc.tensor.transpose(bank(1, c * P, c * P + P, V), st_h[:, S + V * c:S + V * c + V], ident[:, :])
                        nc.tensor.transpose(bank(0, 0, P, S), st_h[:, 0:S], ident[:, :]).then_inc(n_turned, 1)
                        pe.wait_ge(n_copied, i + (BLOCKS + 1))
                        if not first:
                            pe.wait_ge(n_mixed_copied, i + BLOCKS)
                        mm(bank(2, 0, S), s_t, wt("lin_s"), start=True, stop=True, skip_group_check=True)
                        for c in range(3):
                            t = mm(bank(2, S + V * c, S + V * c + V), v_t[:, c * P:c * P + P], wt("lin_v"),
                                   start=False, stop=True, skip_group_check=True)
                        t.then_inc(n_mixed, 1)

                    turns(pe, BLOCKS, project)
                meet(pe, phase_no(layer, K_NORM))

                def scatter(i, s, j, first):
                    pair = 2 * s + j
                    if not (first and pair < 2 and layer == 0):
                        pe.wait_ge(added, i * (2 * SLOTS) + (PAIRS * layer + pair - 1))
                    acc = psum[:, (pair % 2) * 2 * BANK:(pair % 2) * 2 * BANK + 2 * BANK]
                    slot = s % SLOTS

                    def into(lo, n):
                        return acc[:, lo:lo + n]

                    def vec(lo):
                        return acc[:, 0:3 * P].rearrange("p (c n) -> p c n", n=P)[:, :, lo:lo + V]

                    for t in range(2 * j, 2 * j + 2):
                        kind = [hot[:, slot % 2, t, k, :] for k in range(KINDS)]
                        todo = []
                        if layer in (0, 2):
                            r = rows_x[:, slot, t, :]
                            sc, ve = r[:, 0:S], r[:, S:F]
                            vv = ve.rearrange("p (c n) -> p c n", n=V)
                            todo += [(into(3 * P, S), kind[3], sc), (vec(S), kind[3], vv),
                                     (into(3 * P + S, S), kind[4], sc), (vec(96), kind[4], vv)]
                            for c in range(3):
                                todo += [(into(c * P, S), kind[c], sc), (into(4 * P, V), kind[c], ve[:, c * V:c * V + V])]
                        else:
                            s1, v3, s2, pos, ngt, dot = parts(layer, slot, t)
                            todo += [(into(3 * P, S), kind[0], s1), (vec(S), kind[0], v3.rearrange("p (c n) -> p c n", n=V))]
                            for m in range(3):
                                k1, k2 = (m + 1) % 3, (m + 2) % 3
                                todo += [(into(m * P, S), kind[1 + m], s2),
                                         (into(3 * P + S, V), kind[1 + m], dot[:, m * V:m * V + V]),
                                         (into(k1 * P + 96, V), kind[1 + m], pos[:, k2 * V:k2 * V + V]),
                                         (into(k2 * P + 96, V), kind[1 + m], ngt[:, k1 * V:k1 * V + V])]
                        for n, (o, l, r) in enumerate(todo):
                            opens = t == 2 * j and (n == 0 or (layer in (0, 2) and n == 5))
                            last = mm(o, l, r, start=opens, stop=(t == 2 * j + 1 and n == len(todo) - 1), skip_group_check=True)
                    last.then_inc(scattered, 1)

                if layer == 1:
                    def edges(i, first):
                        for s in range(SLOTS):
                            nth = s + 1
                            pe.wait_ge(x_ready[s], i * 64 + 64 * (TURNS * layer + 1))
                            if not (first and s == 0):
                                pe.wait_ge(msg_ready, i * SLOTS + s)
                                scatter(i, s - 1, 0, first)
                            for t in range(GROUP):
                                tr = nc.tensor.transpose(bank(4, t * P, t * P + P, R_), rec_d[:, s, t, 6:REC_D], ident[:, :])
                            tr.then_inc(es_turned, 1)
                            pe.wait_ge(es_copied, 1)
                            pe.sem_clear(es_copied)
                            mm(bank(5, 0, BANK, R_), wt("fc1"), es_t, start=True, stop=True).then_inc(hid_ready, 1)
                            if not (first and s == 0):
                                scatter(i, s - 1, 1, first)
                            pe.wait_ge(hid_copied, i * SLOTS + nth)
                            fc = small[0:R_, w["fc_a"][0]:w["fc_a"][0] + 256]
                            for t in range(GROUP):
                                last = mm(bank(6 + t // 2, 256 * (t % 2), 256 * (t % 2) + 256), hid[:, t * P:t * P + P], fc,
                                          start=(t % 2 == 0), stop=True, skip_group_check=True)
                            last.then_inc(w_ready, 1)

                    turns(pe, TURNS, edges)
                    pe.wait_ge(msg_ready, GROUPS)
                    scatter(TURNS, -1, 0, False)
                    scatter(TURNS, -1, 1, False)
                else:
                    def edges(i, first):
                        for s in range(SLOTS):
                            pe.wait_ge(hot_ready, i * SLOTS + (GROUPS * layer + s + 1))
                            if layer == 3:
                                pe.wait_ge(neg_ready, i * SLOTS + (s + 1))
                            scatter(i, s, 0, first)
                            scatter(i, s, 1, first)

                    turns(pe, TURNS, edges)
                meet(pe, phase_no(layer, K_EDGE))
                nth = NODE_TURNS[layer]

                def node(i, first):
                    pe.wait_ge(n_staged, i + (nth + 1))
                    tr = nc.tensor.transpose
                    for c in range(3):
                        tr(bank(0, c * P, c * P + P), st_g[:, c * P:c * P + P], ident[:, :])
                    if layer in (0, 2):
                        tr(bank(0, 3 * P, 4 * P), st_g[:, 3 * P:4 * P], ident[:, :])
                        tr(bank(1, 0, P, V), st_g[:, 4 * P:4 * P + V], ident[:, :])
                    else:
                        tr(bank(0, 3 * P, 4 * P, 96), st_g[:, 3 * P:3 * P + 96], ident[:, :])
                    tr(bank(1, P, 2 * P, S), st_h[:, 0:S], ident[:, :])
                    for c in range(3):
                        last = tr(bank(2, c * P, c * P + P, V), st_h[:, S + c * V:S + c * V + V], ident[:, :])
                    last.then_inc(n_turned, 1)
                    pe.wait_ge(n_copied, i + (nth + 1))
                    if layer in (0, 2):
                        k = str(layer)
                        mm(bank(3, 0, S), g_t[:, 3 * P:4 * P], wt("s" + k), start=True, stop=False, skip_group_check=True)
                        mm(bank(3, 0, S), d_t, wt("d" + k), start=False, stop=False, skip_group_check=True)
                        for c in range(3):
                            mm(bank(3, S + c * V, S + c * V + V), g_t[:, c * P:c * P + P], wt("v" + k), start=False, stop=False, skip_group_check=True)
                        mm(bank(3, F, F + P, S), wt("s" + k), g_t[:, 3 * P:4 * P], start=False, stop=False, skip_group_check=True)
                        mm(bank(3, F, F + P, S), wt("d" + k), d_t, start=False, stop=True, skip_group_check=True).then_inc(n_mixed, 1)
                        pe.wait_ge(n_mixed_copied, i + (nth + 1))
                        if not first:
                            pe.wait_ge(n_prod, i + BLOCKS_BEFORE[layer])
                        for c in range(2):
                            mm(bank(4 + c), s_t, w_sv[0:S, c * BANK:c * BANK + BANK], start=True, stop=True)
                        for c in range(2):
                            last = mm(bank(6 + c), agg_t[0:S, 0:P], w_vs[0:S, c * BANK:c * BANK + BANK], start=True, stop=True)
                        last.then_inc(n_partial, 1)
                        upd = bank(3)
                        mm(upd[:, 0:S], s_t, wt("us" + k), start=True, stop=False, skip_group_check=True)
                        for c in range(3):
                            mm(upd[:, S + c * V:S + c * V + V], v_t[:, c * P:c * P + P], wt("uv" + k), start=False, stop=False, skip_group_check=True)
                        for c in range(11):
                            if c < 10:
                                if c < 8:
                                    pe.wait_ge(n_outer_ss, i + (BLOCKS * (layer // 2) + 1))
                                else:
                                    pe.wait_ge(n_outer_vv, i + (BLOCKS * (layer // 2) + 1))
                                if c >= 2:
                                    pe.wait_ge(n_z_copied, i * 10 + (10 * BLOCKS * (layer // 2) + c - 1))
                                for q in range(4):
                                    n = 4 * c + q
                                    last = tr(bank(c % 2, q * P, q * P + P), outer[:, n * P:n * P + P], ident[:, :])
                                last.then_inc(n_z_turned, 1)
                            if c >= 1:
                                pe.wait_ge(n_z_copied, i * 10 + (10 * BLOCKS * (layer // 2) + c))
                                for q in range(4):
                                    n = 4 * (c - 1) + q
                                    mm(upd[:, 0:S], outer_t[:, (c - 1) % 2, q * P:q * P + P], w_outer[:, n * S:n * S + S],
                                       start=False, stop=False, skip_group_check=True)
                        pe.wait_ge(n_prod, i + (BLOCKS_BEFORE[layer] + 1))
                        for k2 in range(2):
                            for u in range(V):
                                last = mm(upd[:, S:F], ident[:, :], prod[:, k2, u * 96:u * 96 + 96], start=False,
                                          stop=(k2 == 1 and u == V - 1), skip_group_check=True)
                        last.then_inc(n_summed, 1)
                    if layer == 1:
                        mm(bank(3, 0, 96), g_t[0:96, 3 * P:4 * P], wt("out_s"), start=True, stop=False, skip_group_check=True)
                        mm(bank(3, 0, 96), s_t, wt("sc_s"), start=False, stop=False, skip_group_check=True)
                        for c in range(3):
                            o = bank(3, 96 + c * V, 96 + c * V + V)
                            mm(o, g_t[:, c * P:c * P + P], wt("out_v"), start=False, stop=False, skip_group_check=True)
                            last = mm(o, v_t[:, c * P:c * P + P], wt("sc_v"), start=False, stop=(c == 2), skip_group_check=True)
                        last.then_inc(n_mixed, 1)
                    if layer == 3:
                        mm(bank(3, 0, P, S), wt("m_s"), g_t[0:96, 3 * P:4 * P], start=True, stop=True, skip_group_check=True)
                        last = mm(bank(3, P, 4 * P, V), wt("m_v"), g_t[:, 0:3 * P], start=True, stop=True, skip_group_check=True)
                        last.then_inc(n_mixed, 1)
                        pe.wait_ge(n_mixed_copied, i + (nth + 1))
                        mm(bank(4, 0, S), agg_t[0:S, 0:P], wt("h_s"), start=True, stop=False, skip_group_check=True)
                        for c in range(3):
                            last = mm(bank(4, S + c * V, S + c * V + V), agg_t[0:V, P + c * P:P + c * P + P], wt("h_v"),
                                      start=False, stop=(c == 2), skip_group_check=True)
                        last.then_inc(n_summed, 1)

                turns(pe, BLOCKS, node)
                meet(pe, phase_no(layer, K_NODE))

        @block.vector
        def _(dve):
            step = Steps(dve, v_step)
            tt, ts, stt = nc.vector.tensor_tensor, nc.vector.tensor_scalar, nc.vector.scalar_tensor_tensor
            f3 = fill.rearrange("p (n r) -> p n r", r=REC_D)
            step(nc.vector.memset(fill, 0.0))
            nc.vector.memset(f3[:, :, 1:2], -1.0).then_inc(fill_ready, 1)
            f3 = fill_s.rearrange("p (n r) -> p n r", r=REC_S)
            step(nc.vector.memset(fill_s, 0.0))
            nc.vector.memset(f3[:, :, 1:2], -1.0).then_inc(fill_ready, 1)
            step(nc.vector.memset(zero, 0.0))
            dve.wait_ge(loaded, 64)
            dve.wait_ge(consts_ready, 6)
            for k in range(2):
                step(ts(temp_i, key[k], 7, None, ALU.logical_shift_right))
                step(nc.vector.tensor_copy(blk, temp_i))
                step(ts(temp_i, key[k], P - 1, None, ALU.bitwise_and))
                step(nc.vector.tensor_copy(loc[k], temp_i))
                step(nc.vector.memset(rank, 0.0))

                def ranks(i, first):
                    step.at(ts(is_b, blk, bucket_no[:, bass.ds(i, 1)], None, ALU.is_equal), i, 1, 5)
                    step.at(nc.vector.tensor_tensor_scan(upto, is_b, zero, 0.0, ALU.add, ALU.add), i, 2, 5)
                    step.at(nc.vector.tensor_copy(count[:, bass.ds(i, 1)], upto[:, COLS - 1:COLS]), i, 3, 5)
                    step.at(tt(upto, upto, is_b, ALU.mult), i, 4, 5)
                    step.at(tt(rank, rank, upto, ALU.add), i, 5, 5)

                turns(dve, BUCKETS, ranks)
                step.n += 5 * BUCKETS
                dve.engine_nop().then_inc(counted, 1)
                dve.wait_ge(prefixed, k + 1)
                step(ts(total_i, bank(1, 0, BUCKETS), float(PAIR - 1), None, ALU.add))
                step(ts(total_i, total_i, PAIR.bit_length() - 1, None, ALU.logical_shift_right))
                step(nc.vector.tensor_copy(supers, total_i))
                step(nc.vector.tensor_tensor_scan(ends, supers, zero[:, 0:BUCKETS], 0.0, ALU.add, ALU.add))
                step(tt(start, ends, supers, ALU.subtract))
                step(nc.vector.memset(start[:, BLOCKS:BUCKETS], float(PAIRS)))
                step(ts(start, start, float(PAIR), -1.0, ALU.mult, ALU.add))
                step(tt(start, start, bank(0, 0, BUCKETS), ALU.add))

                def slots_of(i, first):
                    step.at(ts(is_b, blk, bucket_no[:, bass.ds(i, 1)], start[:, bass.ds(i, 1)], ALU.is_equal, ALU.mult), i, 1, 2)
                    step.at(tt(rank, rank, is_b, ALU.add), i, 2, 2)

                turns(dve, BUCKETS, slots_of)
                step.n += 2 * BUCKETS
                step(nc.vector.tensor_copy(temp_i, rank))
                step(ts(temp_j, temp_i, P - 1, None, ALU.bitwise_and))
                step(ts(temp_i, temp_i, 7, None, ALU.logical_shift_right))
                step(ts(temp_j, temp_j, float(ROW), None, ALU.mult))
                step(tt(addr[k], temp_i, temp_j, ALU.add))
                step(nc.vector.memset(block_of, 0.0))

                def blocks_of(i, first):
                    step.at(stt(block_of, iota_pairs, ends[0:1, bass.ds(i, 1)], block_of, ALU.is_ge, ALU.add), i, 1, 1)

                turns(dve, BLOCKS, blocks_of)
                step.n += BLOCKS
                step(ts(block_of, block_of, float(BLOCKS - 1), float(LAYER_WIDTH[k]), ALU.min, ALU.mult))
                step(nc.vector.tensor_copy([offs_src, offs_dst][k][0:1, :], block_of))
            meet(dve, 1)

            def chunk(i, first):
                for s in range(2):
                    dve.wait_ge(chunk_loaded[s], i * 16 + 16)
                    at = bass.ds((i * 2 + s) * CHUNK, CHUNK)
                    cp = nc.vector.tensor_copy
                    cp(stage_d[:, s, :, 0].bitcast(I32), key[0][:, at])
                    cp(stage_d[:, s, :, 1], loc[1][:, at])
                    cp(stage_s[:, s, :, 0].bitcast(I32), key[1][:, at])
                    cp(stage_s[:, s, :, 1], loc[0][:, at])
                    cp(stage_s[:, s, :, 2:6], stage_d[:, s, :, 2:6])
                    cp(to_s[:, s, :].bitcast(I32), addr[0][:, at])
                    cp(to_d[:, s, :].bitcast(I32), addr[1][:, at]).then_inc(chunk_filled[s], 1)

            turns(dve, CHUNKS // 2, chunk)
            meet(dve, 2)

            x3 = x[:, :].rearrange("p (b f) -> p b f", f=F)
            h3 = h[:, :].rearrange("p (b f) -> p b f", f=F)

            def spread(t):
                return repeat(t.rearrange("p (b o) -> p b o", o=1), 2, F)

            for layer in range(4):
                step(nc.vector.tensor_reduce(mean[:, :], x3, AX_X, ALU.add))
                step(ts(mean[:, :], mean[:, :], 1.0 / F, None, ALU.mult))
                tt(h3, x3, spread(mean[:, :]), ALU.subtract).then_inc(centred, 1)
                dve.wait_ge(squared, layer + 1)
                step(nc.vector.tensor_reduce(var[:, :], square.rearrange("p (b f) -> p b f", f=F), AX_X, ALU.add))
                ts(var[:, :], var[:, :], 1.0 / F, 1e-5, ALU.mult, ALU.add).then_inc(var_ready, 1)
                dve.wait_ge(root_ready, layer + 1)
                step(nc.vector.reciprocal(mean[:, :], var[:, :]))
                step(tt(h3, h3, spread(mean[:, :]), ALU.mult))
                ts(h[:, :], h[:, :], 0.0, None, ALU.max).then_inc(normed, 1)
                meet(dve, phase_no(layer, K_NORM))

                width = LAYER_WIDTH[layer]
                step(nc.vector.memset(sums[:, 0:BLOCKS * width], 0.0))
                rec = rec_s if layer % 2 == 0 else rec_d
                offs = offs_src if layer % 2 == 0 else offs_dst

                def add(i, s, j, first):
                    pair = 2 * s + j
                    where = dve.value_load(offs[0:1, bass.ds(i * (2 * SLOTS) + pair, 1)], min_val=0, max_val=(BLOCKS - 1) * width)
                    blk_sums = sums[:, bass.ds(where, width)]
                    dve.wait_ge(scattered, i * (2 * SLOTS) + (PAIRS * layer + pair + 1))
                    if not (first and pair == 0 and layer == 0):
                        dve.wait_ge(added, i * (2 * SLOTS) + (PAIRS * layer + pair))
                    tt(blk_sums, blk_sums, psum[:, (pair % 2) * 2 * BANK:(pair % 2) * 2 * BANK + width], ALU.add).then_inc(added, 1)

                def edges(i, first):
                    for s in range(SLOTS):
                        dve.wait_ge(x_ready[s], i * 64 + 64 * (TURNS * layer + 1))
                        if not (first and s < 2 and layer == 0):
                            dve.wait_ge(scattered, i * (2 * SLOTS) + (PAIRS * layer + 2 * s - 2))
                        for t in range(GROUP):
                            for k in range(4):
                                last = ts(hot[:, s % 2, t, k, :], iota_row[:, :], rec[:, s, t, 1:2], rec[:, s, t, 2 + k:3 + k],
                                          ALU.is_equal, ALU.mult)
                            if layer in (0, 2):
                                last = ts(hot[:, s % 2, t, 4, :], iota_row[:, :], rec[:, s, t, 1:2], None, ALU.is_equal)
                        last.then_inc(hot_ready, 1)
                        if not (first and s == 0):
                            add(i, s - 1, 0, first)
                            add(i, s - 1, 1, first)
                        if layer == 1:
                            dve.wait_ge(w_ready, i * SLOTS + (s + 1))
                            for t in range(GROUP):
                                wps = bank(6 + t // 2, 256 * (t % 2), 256 * (t % 2) + 256)
                                r = rows_x[:, s, t, :]
                                tt(msg[:, s % 2, t, 0:128].rearrange("p (k n) -> p k n", k=2),
                                   wps[:, 0:128].rearrange("p (k n) -> p k n", k=2),
                                   repeat(r[:, 0:S].rearrange("p (o n) -> p o n", o=1), 1, 2), ALU.mult)
                                last = tt(msg[:, s % 2, t, 128:512].rearrange("p (k c n) -> p k c n", k=4, c=3),
                                          repeat(wps[:, 128:256].rearrange("p (k o n) -> p k o n", k=4, o=1), 2, 3),
                                          repeat(r[:, S:F].rearrange("p (o c n) -> p o c n", o=1, c=3), 1, 4), ALU.mult)
                            last.then_inc(msg_ready, 1)

                turns(dve, TURNS, edges)
                add(TURNS, -1, 0, False)
                add(TURNS, -1, 1, False)
                meet(dve, phase_no(layer, K_EDGE))
                nth = NODE_TURNS[layer]

                def node(i, first):
                    xb = x[:, bass.ds(i * F, F)]
                    if layer in (0, 2):
                        half = BLOCKS * (layer // 2)
                        dve.wait_ge(n_mixed_copied, i + (nth + 1))
                        if not first:
                            dve.wait_ge(n_z_turned, i * 10 + 10 * half)
                        vv = outer[:, 32 * P:40 * P].rearrange("p (u v) -> p u v", v=V)
                        tmp = outer_tmp.rearrange("p (u v) -> p u v", v=V)
                        for c in range(3):
                            u = repeat(st_h[:, S + c * V:S + c * V + V].rearrange("p (u o) -> p u o", o=1), 2, V)
                            v = repeat(agg[:, S + c * V:S + c * V + V].rearrange("p (o v) -> p o v", o=1), 1, V)
                            if c == 0:
                                step.at(tt(vv, u, v, ALU.mult), i, 1, 4)
                            else:
                                step.at(tt(tmp, u, v, ALU.mult), i, 2 * c, 4)
                                t = tt(vv, vv, tmp, ALU.add)
                                if c == 1:
                                    step.at(t, i, 3, 4)
                        t.then_inc(n_outer_vv, 1)
                        dve.wait_ge(n_partial, i + (half + 1))
                        for k in range(2):
                            part = repeat(psum[:, (4 + 2 * k) * BANK:(6 + 2 * k) * BANK].rearrange("p (u o n) -> p u o n", u=V, o=1), 2, 3)
                            by = repeat((agg if k == 0 else st_h)[:, S:F].rearrange("p (c u o) -> p u c o", c=3, o=1), 3, V)
                            last = tt(prod[:, k, :].rearrange("p (u c n) -> p u c n", u=V, c=3), part, by, ALU.mult)
                        last.then_inc(n_prod, 1)
                        dve.wait_ge(n_summed, i + (half + 1))
                        tt(fin[:, 0:F], st_h, bank(3, 0, F), ALU.add).then_inc(n_gated, 1)
                        dve.wait_ge(n_gated, i + (BLOCKS_BEFORE[layer] + 1))
                        tt(xb, xb, fin[:, 0:F], ALU.add).then_inc(n_done, 1)
                    if layer == 1:
                        dve.wait_ge(n_gated, i + (BLOCKS_BEFORE[layer] + 1))
                        g = repeat(st_g[:, 0:V].rearrange("p (o n) -> p o n", o=1), 1, 3)
                        tt(agg[:, S:F].rearrange("p (c n) -> p c n", c=3), fin[:, 96:192].rearrange("p (c n) -> p c n", c=3), g,
                           ALU.mult).then_inc(n_prod, 1)
                        dve.wait_ge(n_prod, i + (BLOCKS + 1))
                        tt(xb, xb, agg, ALU.add).then_inc(n_done, 1)
                    if layer == 3:
                        dve.wait_ge(n_gated, i + (BLOCKS_BEFORE[layer] + 1))
                        tt(fin[:, 0:F], fin[:, 0:F], st_h, ALU.add).then_inc(n_prod, 1)
                        dve.wait_ge(n_prod, i + (BLOCKS_BEFORE[layer] + 1))
                        tt(xb, xb, fin[:, 0:F], ALU.add).then_inc(n_done, 1)

                turns(dve, BLOCKS, node)
                if layer in (0, 2):
                    step.n += 4 * BLOCKS
                meet(dve, phase_no(layer, K_NODE))


def kernel(**inputs):
    import numpy as _np
    import concourse.bacc as _bacc
    from concourse import mybir as _mybir
    from concourse.bass_utils import run_bass_kernel_spmd as _run

    arr = {k: _np.asarray(v) for k, v in inputs.items()}

    def rows(v):
        o = _np.zeros((NODES, v.shape[1]), v.dtype)
        o[:N] = v
        return o

    x = arr["x"]
    vec = x[:, S:].reshape(N, V, C3).transpose(0, 2, 1).reshape(N, C3 * V)
    put = {"x": rows(_np.concatenate([x[:, :S], vec], axis=1)),
           "node_vec1": _np.ascontiguousarray(rows(arr["node_vec1"]).reshape(BLOCKS, P).T)}
    for k in ("src", "dst"):
        o = _np.full((P * COLS,), NODES, arr[k].dtype)
        o[:E] = arr[k]
        put[k] = o.reshape(P, COLS)
    attrs = _np.zeros((P * COLS, 4 + R_), x.dtype)
    attrs[:E, :4] = arr["edge_attr_4"]
    attrs[:E, 4:] = arr["edge_attr_64"]
    put["attrs"] = attrs.reshape(P, COLS, 4 + R_)
    for k, v in arr.items():
        if k[:2] in ("L0", "L1", "L2", "L3"):
            if k[:7] == "L2_gnn_" and k[7:9] == "wm":
                v = v[:, 0, :]
            if k in ("L0_gnn_Wu_ss", "L0_gnn_Wu_vv", "L2_gnn_wu000", "L2_gnn_wu110"):
                v = v.reshape(-1, v.shape[2])
            if k in ("L0_gnn_Wu_sv", "L2_gnn_wu011"):
                v = v.reshape(v.shape[0], -1)
            put[k] = v
    nc = _bacc.Bacc("TRN2", target_bir_lowering=False, num_devices=1)
    arrays, aps = {}, {}
    for name, v in put.items():
        v = _np.ascontiguousarray(v)
        arrays[f"in_{name}"] = v
        aps[name] = nc.dram_tensor(f"in_{name}", v.shape, _mybir.dt.from_np(v.dtype), kind="ExternalInput").ap()
    out = nc.dram_tensor("out_0", (NODES, F), _mybir.dt.float32, kind="ExternalOutput").ap()
    program(nc, aps, out)
    r = _run(nc, [arrays], core_ids=[0])
    got = r.results[0]["out_0"][:N]
    vec = got[:, S:].reshape(N, C3, V).transpose(0, 2, 1).reshape(N, C3 * V)
    return _np.concatenate([got[:, :S], vec], axis=1)
```

```python
from contextlib import ExitStack
from math import sqrt

import concourse.bass as bass
from concourse import mybir

ALU = mybir.AluOpType
ACT = mybir.ActivationFunctionType
AX_X = mybir.AxisListType.X
F32 = mybir.dt.float32
BF16 = mybir.dt.bfloat16
I32 = mybir.dt.int32
U32 = mybir.dt.uint32

P = 128
N = 3125
E = 100000
S, V, C3 = 64, 32, 3
F = S + C3 * V
NB = 25
BLOCKS = N // NB
NT = 125
PER = NT // NB
NTILES = N // NT
GROUP = 4
SLOTS = 4
TILES = -(-(E // P + BLOCKS) // (GROUP * SLOTS)) * (GROUP * SLOTS)
GROUPS = TILES // GROUP
TURNS = GROUPS // SLOTS
COLS = 784
QUADS = COLS // 4
PADS = COLS * P - E
ROW = TILES + -(-PADS // P)
BUCKETS = BLOCKS + 1
REC_S = 6
REC_D = 70
R_ = 64
CHUNK = 14
CHUNKS = COLS // CHUNK
FILL = 61
BANK = 512
ISQ3 = 0.5773502691896258
MSG = 416
assert N == NB * BLOCKS == NT * NTILES and NTILES % 2 == 1
assert COLS * P >= E and QUADS % 4 == 0
assert CHUNKS * CHUNK == COLS and CHUNKS % 2 == 0 and ROW % FILL == 0
assert GROUPS % SLOTS == 0


def program(nc, a, out):
    with ExitStack() as ctx:
        def sb(name, cols, dt=F32, rows=P):
            return ctx.enter_context(nc.sbuf_tensor(name, [rows, cols], dt))

        def sem(name):
            return ctx.enter_context(nc.semaphore(name))

        slots_src = nc.dram_tensor("slots_src", (P * ROW, REC_S), F32, kind="Internal").ap()
        slots_dst = nc.dram_tensor("slots_dst", (P * ROW, REC_D), F32, kind="Internal").ap()
        table = [nc.dram_tensor(f"table{n}", (N, F), F32, kind="Internal").ap() for n in range(4)]

        x = sb("x", NTILES * F)
        h = sb("h", NTILES * F)
        sums = sb("sums", BLOCKS * F)
        scale_a = sb("scale_a", NTILES)
        w_ss = sb("w_ss", S * S)
        w_vv = sb("w_vv", 8 * S)
        w_sv = sb("w_sv", V * V)
        w_vs = sb("w_vs", V * V)
        mix = sb("mix", 2 * 6 * F)
        iota_row = sb("iota_row", P)
        ident = sb("ident", P)
        ones = sb("ones", P)
        ones_b = sb("ones_b", P, BF16)
        before_b = sb("before_b", P, BF16)
        upto_b = sb("upto_b", P, BF16)
        offs_src = sb("offs_src", TILES, I32, 1)
        offs_dst = sb("offs_dst", TILES, I32, 1)
        mean = sb("mean", NTILES)
        var = sb("var", NTILES)

        r96, r32, r128 = 1 / sqrt(96), 1 / sqrt(32), 1 / sqrt(128)
        c0, c1, c6 = 1 / sqrt(S + V), sqrt(3.0 / (S + 2 * V)), 1 / sqrt(6.0)
        small = sb("small", 2 * F + P + 224)
        lin = small[:, 0:2 * F]
        fc1 = small[:, 2 * F:2 * F + P]
        fc2 = small[:, 2 * F + P:]
        lin_v = a["L1_gnn_lin1_wv"]
        loads = [(fc1[r:r + R_, r:r + R_], a["L1_gnn_fc_w1"], 1.0) for r in (0, R_)] + [
                 (fc2[r:r + R_, :], a["L1_gnn_fc_w2"], .125) for r in (0, R_)] + [
                 (lin[0:S, 0:S], a["L1_gnn_lin1_ws"], .125),
                 (lin[S:96, S:96], lin_v, r32), (lin[96:P, 96:P], lin_v, r32), (lin[0:V, F + P:2 * F], lin_v, r32)]

        def vec(c):
            return S + c % 3 * V

        def messages(ss, vv, sv, vs, k_ss, k_vv, k_sv, k_vs):
            return [e for c in range(3) for e in ((c, 0, vec(c), sv, k_sv), (c, vec(c), 0, vv, k_vv), (3, vec(c), vec(c), vs, k_vs))
                    ] + [(3, 0, 0, ss, k_ss)]

        def diagonal(kind, scalars, vectors, k_s, k_v, first=S):
            return [(kind, 0, 0, scalars, k_s)] + [(kind, vec(c), first + c * V, vectors, k_v) for c in range(3)]

        lin2_s, lin2_v = a["L1_gnn_lin2_ws"], a["L1_gnn_lin2_wv"]
        k2s, k2v = .25 * r96, .25 * r128
        mixes = [
            messages(a["L0_gnn_Wm_ss"], a["L0_gnn_Wm_vv"], a["L0_gnn_Wm_sv"], a["L0_gnn_Wm_vs"], .125, ISQ3 * r32, .125, r32)
            + diagonal(4, a["L0_gnn_Lm_s"], a["L0_gnn_Lm_v"], .125, r32) + diagonal(5, a["L0_gnn_Lu_s"], a["L0_gnn_Lu_v"], .125, r32),
            diagonal(3, lin2_s[0:S, :], lin2_v[S:96, :], k2s, k2v, 96)
            + [(m, 0, 96 + m * V, lin2_v[0:S, :], k2v) for m in range(3)]
            + [(m, S + V * piece, 0, lin2_s[S:96, :], k2s / sqrt(3)) for m, piece in ((0, 0), (1, 2), (2, 2))]
            + [(m, S + V * piece, 96 + c * V, lin2_v[96:P, :], sign * k2v / sqrt(2))
               for m, piece, c, sign in ((0, 2, 1, 1), (0, 1, 2, -1), (1, 1, 2, 1), (1, 0, 0, -1), (2, 0, 0, 1), (2, 1, 1, -1))]
            + diagonal(4, a["L1_gnn_sc_ws"], a["L1_gnn_sc_wv"], .125, r32, 96),
            messages(a["L2_gnn_wm000"], a["L2_gnn_wm110"], a["L2_gnn_wm011"], a["L2_gnn_wm101"], r96, ISQ3 * r96, r96, r96)
            + diagonal(4, a["L2_gnn_lm0"], a["L2_gnn_lm1"], .125, r32) + diagonal(5, a["L2_gnn_lu0"], a["L2_gnn_lu1"], .125, r32),
            diagonal(0, a["L3_gnn_W1"], a["L3_gnn_W4"], c0, c1 * ISQ3)
            + [e for m in range(3) for e in (
                (1 + m, 0, vec(m), a["L3_gnn_W3"], c1 * ISQ3), (1 + m, vec(m), 0, a["L3_gnn_W2"], c0 * ISQ3),
                (1 + m, vec(m + 2), vec(m + 1), a["L3_gnn_W5"], c1 * c6), (1 + m, vec(m + 1), vec(m + 2), a["L3_gnn_W5"], -c1 * c6))]
            + diagonal(4, a["L3_gnn_Ws"], a["L3_gnn_Wv"], .125, r32),
        ]
        MIXED = [F, 192, F, F]
        KINDS = [5, 4, 5, 4]
        WIDE = [NB, V, NB, NB]

        def mix_at(layer, kind, row, rows, col, cols):
            n = MIXED[layer]
            c = ((row // P) * (KINDS[layer] + 1) + kind) * n + col
            return mix[row % P:row % P + rows, c:c + cols]

        EDGE_COLS, LATE_COLS = 4480, 6000
        shared = sb("shared", EDGE_COLS + LATE_COLS)

        def repeat(ap, dim, n):
            shape = list(ap.shape)
            shape[dim] = n
            return ap.broadcast_to(shape)

        class Area:
            def __init__(self, tensor, lo=0, hi=None):
                self.t, self.at, self.hi = tensor, lo, hi or tensor.shape[1]

            def take(self, cols, rows=P):
                v = self.t[0:rows, self.at:self.at + cols]
                self.at += cols
                assert self.at <= self.hi, (self.at, self.hi)
                return v

        area = Area(shared, 0, EDGE_COLS)
        rec_s = area.take(SLOTS * GROUP * REC_S).rearrange("p (s t r) -> p s t r", s=SLOTS, t=GROUP)
        rows_x = area.take(SLOTS * GROUP * F).rearrange("p (s t f) -> p s t f", s=SLOTS, t=GROUP)
        hot = area.take(2 * GROUP * P).rearrange("p (s t n) -> p s t n", s=2, t=GROUP)
        one_hot = area.take(2 * GROUP * V).rearrange("p (s t n) -> p s t n", s=2, t=GROUP)
        area = Area(shared, EDGE_COLS)
        rec_d = area.take(SLOTS * GROUP * REC_D).rearrange("p (s t r) -> p s t r", s=SLOTS, t=GROUP)
        msg = area.take(2 * GROUP * MSG).rearrange("p (s t f) -> p s t f", s=2, t=GROUP)
        es_t = area.take(2 * P)
        hid = area.take(2 * P)
        es_s = area.take(2 * P).rearrange("p (j d r) -> p j d r", j=2, d=2)
        area = Area(shared, EDGE_COLS)
        key = [area.take(COLS).bitcast(I32) for _ in range(2)]
        loc1 = area.take(COLS)
        addr1 = area.take(COLS).bitcast(I32)
        stage_d = area.take(2 * CHUNK * REC_D).rearrange("p (s c r) -> p s c r", s=2, c=CHUNK)
        stage_s = area.take(2 * CHUNK * REC_S).rearrange("p (s c r) -> p s c r", s=2, c=CHUNK)
        to = area.take(2 * CHUNK).bitcast(U32).rearrange("p (s c) -> p s c", s=2)
        area = Area(shared, 0, EDGE_COLS)
        st_g = area.take(PER * F)
        st_h = area.take(F)
        g_lo = area.take(2 * PER * P).rearrange("p (s n) -> p s n", s=2)
        g_hi = area.take(2 * PER * P, V).rearrange("p (s n) -> p s n", s=2)
        h_t = area.take(4 * NT).rearrange("p (s n) -> p s n", s=2)
        fin = area.take(192)
        gate = area.take(96)
        st_a = area.take(2)
        area = Area(shared, EDGE_COLS)
        agg_t = area.take(2 * NT)
        agg_s = area.take(F)
        relu = area.take(F)
        area = Area(shared, 0, EDGE_COLS)
        b_agg = area.take(2 * F).rearrange("p (s n) -> p s n", s=2)
        b_h = area.take(2 * F).rearrange("p (s n) -> p s n", s=2)
        b_t = area.take(4 * NT, S).rearrange("p (s n) -> p s n", s=2)
        b_red = area.take(2 * F).rearrange("p (s n) -> p s n", s=2)
        area = Area(sums, NTILES * F)
        prod_ss = area.take(S * S)
        prod_sv = area.take(3 * V * V)
        prod_vs = area.take(3 * V * V)
        pairs_vv = area.take(V * V)
        pairs_tmp = area.take(V * V)
        pairs_t = area.take(8 * NT)
        area = Area(sums)
        square = area.take(NTILES * F)
        proj = area.take(NTILES * F)
        loc = [area.take(COLS), loc1]
        addr = [area.take(COLS).bitcast(I32), addr1]
        blk = area.take(COLS)
        temp_f = area.take(COLS)
        temp_i = area.take(COLS).bitcast(I32)
        temp_j = area.take(COLS).bitcast(I32)
        slot_of = area.take(COLS)
        found = area.take(4 * BUCKETS)
        zero = area.take(BUCKETS)
        total = area.take(BUCKETS)
        total_i = area.take(BUCKETS).bitcast(I32)
        tiles_in = area.take(BUCKETS)
        ends = area.take(BUCKETS)
        ends_col = area.take(1)
        start = area.take(4 * BUCKETS).rearrange("p (q b) -> p q b", q=4)
        iota_tiles = area.take(TILES)
        behind = area.take(TILES)
        fill = shared[:, 0:FILL * REC_D]
        fill_s = area.take(FILL * REC_S)
        in_bucket = sb("in_bucket", 4 * 4 * BUCKETS, BF16)
        in_b = in_bucket[:, :].rearrange("p (s q b) -> p s q b", s=4, q=4)

        psum = ctx.enter_context(nc.psum_tensor("psum", [P, 8 * BANK], F32))

        def bank(n, lo=0, hi=BANK, rows=P):
            return psum[0:rows, n * BANK + lo:n * BANK + hi]

        consts_ready = sem("consts_ready")
        loaded = sem("loaded")
        weights_loaded = sem("weights_loaded")
        outer_loaded = [sem("outer_loaded0"), sem("outer_loaded2")]
        mix_zeroed = sem("mix_zeroed")
        mix_loaded = sem("mix_loaded")
        fill_ready = sem("fill_ready")
        filled_dram = sem("filled_dram")
        v_step = sem("v_step")
        p_step = sem("p_step")
        in_ready = sem("in_ready")
        in_used = sem("in_used")
        ends_ready = sem("ends_ready")
        ends_turned = sem("ends_turned")
        behind_ready = sem("behind_ready")
        behind_summed = sem("behind_summed")
        ranked = sem("ranked")
        slots_found = sem("slots_found")
        addr_ready = sem("addr_ready")
        chunk_loaded = [sem(f"chunk_loaded{s}") for s in range(2)]
        chunk_filled = [sem(f"chunk_filled{s}") for s in range(2)]
        chunk_scattered = [sem(f"chunk_scattered{s}") for s in range(2)]
        all_met = sem("all_met")
        trio_met = sem("trio_met")
        centred = sem("centred")
        squared = sem("squared")
        var_ready = sem("var_ready")
        root_ready = sem("root_ready")
        normed = sem("normed")
        rows_ready = sem("rows_ready")
        table_written = sem("table_written")
        rec_ready = [sem(f"rec_ready{s}") for s in range(SLOTS)]
        x_ready = [sem(f"x_ready{s}") for s in range(SLOTS)]
        eq_ready = sem("eq_ready")
        hot_ready = sem("hot_ready")
        scattered = sem("scattered")
        added = sem("added")
        es_staged = sem("es_staged")
        es_turned = sem("es_turned")
        es_copied = sem("es_copied")
        hid_ready = sem("hid_ready")
        hid_copied = sem("hid_copied")
        w_ready = sem("w_ready")
        msg_ready = sem("msg_ready")
        p_staged = sem("p_staged")
        p_turned = sem("p_turned")
        p_copied = sem("p_copied")
        p_mixed = sem("p_mixed")
        p_done = sem("p_done")
        n_staged = sem("n_staged")
        n_turned = sem("n_turned")
        n_low = sem("n_low")
        n_high = sem("n_high")
        n_mixed = sem("n_mixed")
        n_agg = sem("n_agg")
        n_agg_turned = sem("n_agg_turned")
        n_agg_copied = sem("n_agg_copied")
        n_out = sem("n_out")
        n_fin = sem("n_fin")
        n_gated = sem("n_gated")
        n_scaled = sem("n_scaled")
        n_done = sem("n_done")
        b_staged = sem("b_staged")
        b_turned = sem("b_turned")
        b_copied = sem("b_copied")
        b_chunk = sem("b_chunk")
        b_used = sem("b_used")
        b_pairs = sem("b_pairs")
        b_pairs_turned = sem("b_pairs_turned")
        b_pairs_copied = sem("b_pairs_copied")
        b_summed = sem("b_summed")
        b_upd = sem("b_upd")
        b_fin = sem("b_fin")
        b_done = sem("b_done")
        stored = sem("stored")

        block = ctx.enter_context(nc.Block())

        class Steps:

            def __init__(self, eng, s):
                self.eng, self.sem, self.n = eng, s, 0

            def __call__(self, ins):
                ins.then_inc(self.sem, 1)
                self.n += 1
                self.eng.wait_ge(self.sem, self.n)

            def at(self, ins, t, k, per):
                ins.then_inc(self.sem, 1)
                self.eng.wait_ge(self.sem, t * per + (self.n + k))

        def meet_all(eng, k):
            eng.drain().then_inc(all_met, 1)
            eng.wait_ge(all_met, 5 * k)

        def meet_trio(eng, k):
            eng.drain().then_inc(trio_met, 1)
            eng.wait_ge(trio_met, 3 * k)

        def norm_end(layer):
            return 2 * layer + 1

        def edge_end(layer):
            return 2 * layer + 2

        MIX_END, PROD_END = [1, 3, 4, 6], [2, 3, 5, 6]
        MIX_LOADS = [0]
        for m in mixes:
            MIX_LOADS.append(MIX_LOADS[-1] + len(m))

        def turns(eng, n, body):
            body(0, True, False)
            with eng.Fori(1, n - 1) as i:
                body(i, False, False)
            body(n - 1, False, True)

        def tiles(eng, body):
            def known(t):
                return lambda d: 0 <= t + d < NTILES

            for t in (0, 1):
                body(t, t % 2, known(t))
            with eng.Fori(0, (NTILES - 3) // 2) as i:
                for s in range(2):
                    body(i * 2 + (2 + s), s, lambda d: True)
            for t in range(NTILES - 1, NTILES + 2):
                body(t, t % 2, known(t))

        def vector_pairs(engine, step, t, par):
            pairs = pairs_vv[0:NT, :].rearrange("p (u v) -> p u v", v=V)
            tmp = pairs_tmp[0:NT, :].rearrange("p (u v) -> p u v", v=V)
            for c in range(3):
                u = repeat(b_h[0:NT, par, S + c * V:S + c * V + V].rearrange("p (u o) -> p u o", o=1), 2, V)
                v = repeat(b_agg[0:NT, par, S + c * V:S + c * V + V].rearrange("p (o v) -> p o v", o=1), 1, V)
                if c == 0:
                    step.at(engine.tensor_tensor(pairs, u, v, ALU.mult), t, 1, 4)
                else:
                    step.at(engine.tensor_tensor(tmp, u, v, ALU.mult), t, 2 * c, 4)
                    summed = engine.tensor_tensor(pairs, pairs, tmp, ALU.add)
                    if c == 1:
                        step.at(summed, t, 3, 4)
            summed.then_inc(b_pairs, 1)

        def three(ap):
            return ap.rearrange("p (c n) -> p c n", n=V)

        @block.sync
        def _(sp):
            sp.dma_start(key[0], a["src"]).then_inc(loaded, 16)
            sp.dma_start(key[1], a["dst"]).then_inc(loaded, 16)
            sp.dma_start(x[0:NT, :].rearrange("p (b f) -> p b f", f=F),
                         a["x"].rearrange("(b p) f -> p b f", p=NT)).then_inc(loaded, 16)
            sp.dma_start(scale_a[0:NT, :], a["node_vec1"]).then_inc(loaded, 16)
            sp.wait_ge(fill_ready, 2)
            sp.dma_start(slots_src.rearrange("(p k n) r -> p k (n r)", p=P, n=FILL),
                         repeat(fill_s.rearrange("p (o c) -> p o c", o=1), 1, ROW // FILL)).then_inc(filled_dram, 16)
            sp.dma_start(slots_dst.rearrange("(p k n) r -> p k (n r)", p=P, n=FILL),
                         repeat(fill.rearrange("p (o c) -> p o c", o=1), 1, ROW // FILL)).then_inc(filled_dram, 16)
            for dst, src, _ in loads:
                sp.dma_start(dst, src).then_inc(weights_loaded, 16)

            def load_outer(k):
                n = ("L0_gnn_Wu_ss", "L0_gnn_Wu_vv", "L0_gnn_Wu_sv", "L0_gnn_Wu_vs") if k == 0 else \
                    ("L2_gnn_wu000", "L2_gnn_wu110", "L2_gnn_wu011", "L2_gnn_wu101")
                sp.dma_start(w_ss[0:S, :].rearrange("v (u w) -> v u w", w=S),
                             a[n[0]].rearrange("u v w -> v u w")).then_inc(outer_loaded[k], 16)
                sp.dma_start(w_vv[:, :].rearrange("p (c w) -> p c w", w=S),
                             a[n[1]].rearrange("(c p) w -> p c w", p=P)).then_inc(outer_loaded[k], 16)
                sp.dma_start(w_sv[0:S, :], a[n[2]]).then_inc(outer_loaded[k], 16)
                sp.dma_start(w_vs[0:S, :].rearrange("v (u w) -> v u w", w=V),
                             a[n[3]].rearrange("u v w -> v u w")).then_inc(outer_loaded[k], 16)

            load_outer(0)
            sp.wait_ge(filled_dram, 32)

            def load_attributes(k):
                def chunk(i, first, last):
                    for s in range(2):
                        if not first:
                            sp.wait_ge(chunk_scattered[s], i * (CHUNK * 16) + COLS * 8 * k)
                        at = bass.ds((i * 2 + s) * CHUNK, CHUNK)
                        if k == 0:
                            sp.dma_start(stage_s[:, s, :, 2:REC_S], a["attrs_4"][:, at, :]).then_inc(chunk_loaded[s], 16)
                        else:
                            sp.dma_start(stage_d[:, s, :, 2:REC_D], a["attrs"][:, at, :]).then_inc(chunk_loaded[s], 16)

                turns(sp, CHUNKS // 2, chunk)
                for s in range(2):
                    sp.wait_ge(chunk_scattered[s], COLS * 8 * (k + 1))

            load_attributes(0)

            for layer in range(4):
                sp.wait_ge(rows_ready, layer + 1)
                rows = proj[0:NT, :] if layer == 1 else h[0:NT, :]
                sp.dma_start(table[layer].rearrange("(b p) f -> p b f", p=NT),
                             rows.rearrange("p (b f) -> p b f", f=F)).then_inc(table_written, 16)
                sp.wait_ge(table_written, 16 * (layer + 1))
                meet_all(sp, norm_end(layer))
                sp.wait_ge(mix_zeroed, layer + 1)
                for kind, row, col, src, _ in mixes[layer]:
                    sp.dma_start(mix_at(layer, kind, row, src.shape[0], col, src.shape[1]), src).then_inc(mix_loaded, 16)
                if layer == 1:
                    load_outer(1)
                slots, rec, width = (slots_src, rec_s, REC_S) if layer % 2 == 0 else (slots_dst, rec_d, REC_D)
                slots = slots.rearrange("(p t) r -> p (t r)", p=P)

                def load(i, first, last):
                    for s in range(SLOTS):
                        if not first:
                            if layer == 1:
                                sp.wait_ge(msg_ready, i * SLOTS + (s + 1 - SLOTS))
                            else:
                                sp.wait_ge(scattered, i * SLOTS + (GROUPS * layer + s + 1 - SLOTS))
                        sp.dma_start(rec[:, s, :, :].rearrange("p t r -> p (t r)"),
                                     slots[:, bass.ds((i * SLOTS + s) * (GROUP * width), GROUP * width)]).then_inc(rec_ready[s], 16)

                turns(sp, TURNS, load)
                meet_all(sp, edge_end(layer))
                if layer == 0:
                    load_attributes(1)
            sp.wait_ge(trio_met, 3 * PROD_END[3])
            sp.dma_start(out.rearrange("(b p) f -> p b f", p=NT),
                         x[0:NT, :].rearrange("p (b f) -> p b f", f=F)).then_inc(stored, 16)
            sp.wait_ge(stored, 16)

        @block.gpsimd
        def _(pool):
            pool.iota(iota_row[:, :], [[1, P]], base=0, channel_multiplier=0,
                      allow_small_or_imprecise_dtypes=True).then_inc(consts_ready, 1)
            pool.iota(iota_tiles, [[1, TILES]], base=0, channel_multiplier=0,
                      allow_small_or_imprecise_dtypes=True).then_inc(consts_ready, 1)
            pool.memset(ones[:, :], 1.0).then_inc(consts_ready, 1)
            pool.memset(ones_b[:, :], 1.0).then_inc(consts_ready, 1)
            pool.wait_ge(consts_ready, 4)
            pool.affine_select(out=ident[:, :], in_=ones[:, :], compare_op=ALU.is_equal, fill=0.0, base=0,
                               pattern=[[-1, P]], channel_multiplier=1).then_inc(consts_ready, 1)
            pool.affine_select(out=before_b[:, :], in_=ones[:, :], compare_op=ALU.is_gt, fill=0.0, base=0,
                               pattern=[[1, P]], channel_multiplier=-1).then_inc(consts_ready, 1)
            pool.affine_select(out=upto_b[:, :], in_=ones[:, :], compare_op=ALU.is_ge, fill=0.0, base=0,
                               pattern=[[-1, P]], channel_multiplier=1).then_inc(consts_ready, 1)

            def scatter_records(k):
                stage = (stage_s, stage_d)[k]
                slots = (slots_src, slots_dst)[k]

                def chunk(i, first, last):
                    for s in range(2):
                        pool.wait_ge(chunk_loaded[s], 16)
                        pool.sem_clear(chunk_loaded[s])
                        at = bass.ds((i * 2 + s) * CHUNK, CHUNK)
                        pool.tensor_copy(stage[:, s, :, 0].bitcast(I32), key[1 - k][:, at])
                        pool.tensor_copy(stage[:, s, :, 1], loc[k][:, at])
                        pool.tensor_copy(to[:, s, :].bitcast(I32), addr[k][:, at]).then_inc(chunk_filled[s], 1)
                        pool.wait_ge(chunk_filled[s], 1)
                        pool.sem_clear(chunk_filled[s])
                        for c in range(CHUNK):
                            pool.indirect_dma_start(out=slots, out_offset=bass.IndirectOffsetOnAxis(ap=to[:, s, c:c + 1], axis=0),
                                                    in_=stage[:, s, c, :], in_offset=None).then_inc(chunk_scattered[s], 16)

                turns(pool, CHUNKS // 2, chunk)

            own = Steps(pool, p_step)
            pool.wait_ge(filled_dram, 32)
            pool.wait_ge(addr_ready, 1)
            scatter_records(0)
            for layer in range(4):
                meet_all(pool, norm_end(layer))
                rec = rec_s if layer % 2 == 0 else rec_d

                def gather(i, first, last):
                    for s in range(SLOTS):
                        pool.wait_ge(rec_ready[s], 16)
                        pool.sem_clear(rec_ready[s])
                        for t in range(GROUP):
                            pool.indirect_dma_start(out=rows_x[:, s, t, :], out_offset=None, in_=table[layer],
                                                    in_offset=bass.IndirectOffsetOnAxis(ap=rec[:, s, t, 0:1].bitcast(U32), axis=0)
                                                    ).then_inc(x_ready[s], 16)

                turns(pool, TURNS, gather)
                meet_all(pool, edge_end(layer))
                if layer == 0:
                    scatter_records(1)
                if layer == 2:
                    def products(t, par, has):
                        if has(0):
                            pool.wait_ge(b_staged, t + (NTILES + 1))
                            pool.wait_ge(b_pairs_turned, t + NTILES)
                            vector_pairs(nc.gpsimd, own, t, par)

                    tiles(pool, products)

        @block.scalar
        def _(act):
            act.wait_ge(weights_loaded, 16 * len(loads))
            for dst, _, k in loads:
                if k != 1.0:
                    nc.scalar.mul(dst, dst, k)

            def scale_outer(k):
                act.wait_ge(outer_loaded[k], 64)
                kss, kvv, kt = (1 / 64, ISQ3 / 32, 1 / sqrt(2048)) if k == 0 else (1 / sqrt(5120), ISQ3 / sqrt(5120), 1 / 64)
                nc.scalar.mul(w_ss[0:S, :], w_ss[0:S, :], kss)
                nc.scalar.mul(w_vv[:, :], w_vv[:, :], kvv)
                nc.scalar.mul(w_sv[0:S, :], w_sv[0:S, :], kt)
                nc.scalar.mul(w_vs[0:S, :], w_vs[0:S, :], kt)

            scale_outer(0)
            for layer in range(4):
                act.wait_ge(centred, layer + 1)
                nc.scalar.activation(square[0:NT, :], h[0:NT, :], ACT.Square).then_inc(squared, 1)
                act.wait_ge(var_ready, layer + 1)
                nc.scalar.activation(var[0:NT, :], var[0:NT, :], ACT.Sqrt).then_inc(root_ready, 1)
                if layer == 1:
                    def project(t, par, has):
                        if has(0):
                            if par == 0 and has(-1) is False:
                                act.wait_ge(normed, layer + 1)
                            if has(-1):
                                act.wait_ge(p_turned, t)
                            if has(-2):
                                act.wait_ge(p_done, t - 1)
                            nc.scalar.copy(st_a[0:NT, par:par + 1], scale_a[0:NT, bass.ds(t, 1)])
                            nc.scalar.copy(st_h[0:NT, :], h[0:NT, bass.ds(t * F, F)]).then_inc(p_staged, 1)
                        if has(-1):
                            act.wait_ge(p_mixed, t)
                            nc.scalar.activation(proj[0:NT, bass.ds((t - 1) * F, F)], bank(4 + (1 - par), 0, F, NT), ACT.Copy,
                                                 scale=st_a[0:NT, 1 - par:2 - par]).then_inc(p_done, 1)
                        if has(0):
                            act.wait_ge(p_turned, t + 1)
                            nc.scalar.copy(h_t[:, par, 0:NT], bank(par, 0, NT))
                            nc.scalar.copy(h_t[0:V, par, NT:2 * NT], bank(2 + par, 0, NT, V)).then_inc(p_copied, 1)

                    tiles(act, project)
                    act.drain().then_inc(rows_ready, 1)
                meet_all(act, norm_end(layer))
                act.wait_ge(mix_loaded, 16 * MIX_LOADS[layer + 1])
                for kind, row, col, src, k in mixes[layer]:
                    part = mix_at(layer, kind, row, src.shape[0], col, src.shape[1])
                    nc.scalar.mul(part, part, k)

                if layer == 1:
                    def stage_wide(slot):
                        nc.scalar.copy(es_s, rec_d[:, slot, :, 6:REC_D].rearrange("p (d j) r -> p j d r", d=2)).then_inc(es_staged, 1)

                    act.wait_ge(x_ready[0], 64 * (TURNS * layer + 1))
                    stage_wide(0)

                    def hidden(i, first, last):
                        for s in range(SLOTS):
                            act.wait_ge(es_turned, i * SLOTS + (s + 1))
                            if not (first and s == 0):
                                act.wait_ge(hid_ready, i * SLOTS + s)
                            nc.scalar.copy(es_t, bank(4, 0, 2 * P)).then_inc(es_copied, 1)
                            if not (last and s == SLOTS - 1):
                                act.wait_ge(x_ready[(s + 1) % SLOTS], i * 64 + 64 * (TURNS * layer + 1 + (s + 1) // SLOTS))
                                stage_wide((s + 1) % SLOTS)
                            act.wait_ge(hid_ready, i * SLOTS + (s + 1))
                            if not (first and s == 0):
                                act.wait_ge(w_ready, i * SLOTS + s)
                            nc.scalar.activation(hid, bank(5, 0, 2 * P), ACT.Silu, scale=.125).then_inc(hid_copied, 1)

                    turns(act, TURNS, hidden)
                    scale_outer(1)
                meet_all(act, edge_end(layer))

                base, kinds, wide = NTILES * layer, KINDS[layer], WIDE[layer]
                high = kinds * wide

                def mixing(t, par, has):
                    def stage(u):
                        nc.scalar.copy(st_g[0:high, :], sums[0:high, bass.ds(u * (PER * F), PER * F)])
                        nc.scalar.copy(st_h[0:NT, :], h[0:NT, bass.ds(u * F, F)]).then_inc(n_staged, 1)

                    if has(0) and not has(-1):
                        stage(t)
                    if has(0):
                        act.wait_ge(n_turned, t + (base + 1))
                        if has(-2):
                            act.wait_ge(n_mixed, t + (base - 1))
                        for lo, n, b in ((0, PER - 1, 2), (PER - 1, 1, 3)):
                            nc.scalar.copy(
                                g_hi[:, par, 0:kinds * NT].rearrange("p (k j n) -> p k j n", k=kinds, n=NB)[:, :, lo:lo + n, :],
                                bank(b, 0, n * high, V).rearrange("p (j k n) -> p k j n", k=kinds, n=wide)[:, :, :, 0:NB])
                        nc.scalar.copy(h_t[0:V, par, NT:2 * NT], bank(3, P, P + NT, V)).then_inc(n_high, 1)
                        if has(1):
                            stage(t + 1)
                    if has(-1):
                        o = bank(4 + (1 - par), rows=NT)
                        if layer == 1:
                            act.wait_ge(n_fin, t)
                            if has(-2):
                                act.wait_ge(n_done, t - 1 + base)
                            nc.scalar.activation(gate[0:NT, 0:S], fin[0:NT, 0:S], ACT.Silu)
                            nc.scalar.activation(gate[0:NT, S:96], fin[0:NT, S:96], ACT.Sigmoid).then_inc(n_gated, 1)
                        else:
                            act.wait_ge(n_mixed, t + base)
                            if layer == 3:
                                nc.scalar.copy(agg_s[0:NT, :], o[:, 0:F]).then_inc(n_agg, 1)
                            else:
                                if has(-2):
                                    act.wait_ge(n_done, t - 1 + base)
                                nc.scalar.copy(sums[0:NT, bass.ds((t - 1) * F, F)], o[:, 0:F])
                                nc.scalar.copy(fin[0:NT, 0:F], o[:, F:2 * F]).then_inc(n_agg, 1)
                        if layer == 3:
                            act.wait_ge(n_agg_turned, t)
                            if has(-2):
                                act.wait_ge(n_out, t - 1)
                            nc.scalar.copy(agg_t[:, 0:NT], bank(6, 0, NT))
                            nc.scalar.copy(agg_t[0:V, NT:2 * NT], bank(6, P, P + NT, V)).then_inc(n_agg_copied, 1)
                    if layer == 3 and has(-2):
                        act.wait_ge(n_out, t - 1)
                        if has(-3):
                            act.wait_ge(n_done, t - 2 + base)
                        nc.scalar.activation(relu[0:NT, :], bank(7, 0, F, NT), ACT.Relu).then_inc(n_gated, 1)

                tiles(act, mixing)
                meet_trio(act, MIX_END[layer])
                if layer in (0, 2):
                    half = NTILES * (layer // 2)

                    def products(t, par, has):
                        def stage(u, p, reused):
                            if reused:
                                act.wait_ge(b_used, (u - 1) * 6 + 6 * half)
                                act.wait_ge(b_pairs, (u - 1) + half)
                            nc.scalar.copy(b_agg[0:NT, p, :], sums[0:NT, bass.ds(u * F, F)])
                            nc.scalar.copy(b_h[0:NT, p, :], h[0:NT, bass.ds(u * F, F)]).then_inc(b_staged, 1)

                        if has(0):
                            if not has(-1):
                                stage(t, par, False)
                            act.wait_ge(b_turned, t + (half + 1))
                            nc.scalar.copy(b_t[:, par, :], bank(6, 0, 2 * NT, S)).then_inc(b_copied, 1)
                            act.wait_ge(b_pairs_turned, t + (half + 1))
                            nc.scalar.copy(pairs_t[:, 0:4 * NT], bank(6, 0, 4 * NT))
                            nc.scalar.copy(pairs_t[:, 4 * NT:], bank(7, 0, 4 * NT)).then_inc(b_pairs_copied, 1)
                            if has(1):
                                stage(t + 1, 1 - par, has(-1))

                    tiles(act, products)
                    meet_trio(act, PROD_END[layer])

        @block.tensor
        def _(pe):
            mm, tr = nc.tensor.matmul, nc.tensor.transpose
            pe.wait_ge(consts_ready, 7)
            for k in range(2):
                base = 2 * k * QUADS

                def count(i, first, last):
                    for s in range(4):
                        pe.wait_ge(in_ready, i * 4 + (base + s + 1))
                        mm(bank(0, 0, 4 * BUCKETS), ones_b[:, :], in_b[:, s].rearrange("p q b -> p (q b)"),
                           start=(first and s == 0), stop=(last and s == 3), skip_group_check=True).then_inc(in_used, 1)

                turns(pe, QUADS // 4, count)
                pe.wait_ge(ends_ready, k + 1)
                mm(bank(1, 0, 4 * BUCKETS), ident[:, :], start.rearrange("p q b -> p (q b)"),
                   start=True, stop=False, skip_group_check=True)
                tr(bank(2, 0, P, BUCKETS), ends, ident[:, :]).then_inc(ends_turned, 1)
                pe.wait_ge(behind_ready, k + 1)
                for c in range(2):
                    t = mm(bank(3 + c, 0, TILES // 2), ones[0:BLOCKS, :], behind[0:BLOCKS, c * (TILES // 2):(c + 1) * (TILES // 2)],
                           start=True, stop=True)
                t.then_inc(behind_summed, 1)
                base += QUADS

                def rank(i, first, last):
                    for s in range(4):
                        pe.wait_ge(in_ready, i * 4 + (base + s + 1))
                        mm(bank(1, 0, 4 * BUCKETS), before_b[:, :], in_b[:, s].rearrange("p q b -> p (q b)"),
                           start=False, stop=True, skip_group_check=True).then_inc(ranked, 1)
                        pe.wait_ge(slots_found, i * 4 + (QUADS * k + s + 1))
                        mm(bank(1, 0, 4 * BUCKETS), upto_b[:, :], in_b[:, s].rearrange("p q b -> p (q b)"),
                           start=False, stop=True, skip_group_check=True).then_inc(in_used, 1)

                turns(pe, QUADS // 4, rank)
            pe.wait_ge(weights_loaded, 16 * len(loads))
            for layer in range(4):
                if layer == 1:
                    def project(t, par, has):
                        if has(0):
                            pe.wait_ge(p_staged, t + 1)
                            tr(bank(par, 0, NT), st_h[0:NT, 0:P], ident[0:NT, 0:NT])
                            tr(bank(2 + par, 0, NT, V), st_h[0:NT, P:F], ident[0:NT, 0:NT]).then_inc(p_turned, 1)
                            pe.wait_ge(p_copied, t + 1)
                            if has(-2):
                                pe.wait_ge(p_done, t - 1)
                            linear(bank(4 + par, 0, F, NT), h_t[:, par, :], lin[:, 0:F], lin[0:V, F:2 * F], True).then_inc(p_mixed, 1)

                def linear(o, turned, low, high, opens):
                    mm(o, turned[:, 0:NT], low, start=opens, stop=False, skip_group_check=True)
                    return mm(o, turned[0:V, NT:2 * NT], high, start=False, stop=True, skip_group_check=True)

                def own_rows(layer):
                    k, n = KINDS[layer], MIXED[layer]
                    return mix_at(layer, k, 0, P, 0, n), mix_at(layer, k, P, V, 0, n)

                if layer == 1:
                    tiles(pe, project)
                meet_all(pe, norm_end(layer))

                def scatter(i, s, first, which=range(GROUP)):
                    slot = s % SLOTS
                    if 0 in which and not (first and s < 2 and layer == 0):
                        pe.wait_ge(added, i * (SLOTS * GROUP) + (TILES * layer + GROUP * (s - 1)))
                    for t in which:
                        o = bank(2 * (slot % 2) + t // 2, F * (t % 2), F * (t % 2) + F)
                        opens = t % 2 == 0
                        if layer == 1:
                            m = msg[:, slot % 2, t, :]
                            hs = hot[:, slot % 2, t, :]
                            pieces = m[:, S + F:MSG].rearrange("p (q n) -> p q n", n=V)
                            mm(o[0:96, 0:S], hs[:, V:P], m[:, F:F + S], start=opens, stop=False, skip_group_check=True)
                            mm(o[96:P, :], hs[:, 0:V], m[:, 0:F], start=opens, stop=True, skip_group_check=True)
                            for c, piece in enumerate((pieces[:, 0:3, :], pieces[:, 2:5, :],
                                                       m[:, S + F:MSG].rearrange("p (q b n) -> p b q n", b=2, n=V)[:, 1])):
                                last = mm(three(o[c * V:c * V + V, S:F]), hs[:, V + c * V:2 * V + c * V], piece,
                                          start=False, stop=True, skip_group_check=True)
                        else:
                            n = KINDS[layer] * NB
                            last = mm(o[0:n, :], hot[:, slot % 2, t, 0:n], rows_x[:, slot, t, :], start=opens, stop=True,
                                      skip_group_check=True)
                    if GROUP - 1 in which:
                        last.then_inc(scattered, 1)

                if layer == 1:
                    def turn_wide():
                        for j in range(2):
                            turned = tr(bank(4, j * P, j * P + P), es_s[:, j].rearrange("p d r -> p (d r)"), ident[:, :])
                        turned.then_inc(es_turned, 1)

                    def edges(i, first, last_turn):
                        for s in range(SLOTS):
                            old = not (first and s < 2)
                            if old:
                                scatter(i, s - 2, first, (0, 1))
                            pe.wait_ge(es_copied, 1)
                            pe.sem_clear(es_copied)
                            mm(bank(5, 0, 2 * P), fc1, es_t, start=True, stop=True).then_inc(hid_ready, 1)
                            if old:
                                scatter(i, s - 2, first, (2, 3))
                            pe.wait_ge(hid_copied, i * SLOTS + (s + 1))
                            if not (first and s == 0):
                                pe.wait_ge(msg_ready, i * SLOTS + s)
                            more = not (last_turn and s == SLOTS - 1)
                            if more:
                                pe.wait_ge(es_staged, i * SLOTS + (s + 2))
                            for t in (0, 2, 1, 3):
                                part = slice(t // 2 * R_, t // 2 * R_ + R_)
                                last = mm(bank(6 + t // 2, 256 * (t % 2), 256 * (t % 2) + 224), hid[part, t % 2 * P:t % 2 * P + P],
                                          fc2[part, :], start=(t % 2 == 0), stop=True, skip_group_check=True)
                            last.then_inc(w_ready, 1)
                            if more:
                                turn_wide()

                    pe.wait_ge(es_staged, 1)
                    turn_wide()
                    turns(pe, TURNS, edges)
                    pe.wait_ge(msg_ready, GROUPS)
                    scatter(TURNS, -2, False)
                    scatter(TURNS, -1, False)
                else:
                    def edges(i, first, last_turn):
                        for s in range(SLOTS):
                            pe.wait_ge(hot_ready, i * SLOTS + (GROUPS * [0, 0, 1, 2][layer] + s + 1))
                            scatter(i, s, first)

                    turns(pe, TURNS, edges)
                meet_all(pe, edge_end(layer))
                base, kinds, wide = NTILES * layer, KINDS[layer], WIDE[layer]
                high, cols = kinds * wide, MIXED[layer]

                def mixing(t, par, has):
                    def turn(u, earlier):
                        pe.wait_ge(n_staged, u + (base + 1))
                        if earlier:
                            pe.wait_ge(n_low, u + base)
                            pe.wait_ge(n_high, u + base)
                        for j in range(PER):
                            at = (j % 4) * high
                            tr(bank(j // 4, at, at + high), st_g[0:high, j * F:j * F + P], ident[0:high, 0:high])
                            tr(bank(2 + j // 4, at, at + high, V), st_g[0:high, j * F + P:j * F + F], ident[0:high, 0:high])
                        tr(bank(1, P, P + NT), st_h[0:NT, 0:P], ident[0:NT, 0:NT])
                        tr(bank(3, P, P + NT, V), st_h[0:NT, P:F], ident[0:NT, 0:NT]).then_inc(n_turned, 1)

                    if has(0) and not has(-1):
                        turn(t, False)
                    if has(1):
                        turn(t + 1, True)
                    if layer == 3 and has(-1):
                        pe.wait_ge(n_agg, t + 2 * NTILES)
                        tr(bank(6, 0, NT), agg_s[0:NT, 0:P], ident[0:NT, 0:NT])
                        tr(bank(6, P, P + NT, V), agg_s[0:NT, P:F], ident[0:NT, 0:NT]).then_inc(n_agg_turned, 1)
                    if has(0):
                        pe.wait_ge(n_low, t + (base + 1))
                        pe.wait_ge(n_high, t + (base + 1))
                        if has(-2):
                            pe.wait_ge(n_fin, t - 1) if layer == 1 else pe.wait_ge(n_agg, t - 1 + NTILES * [0, 0, 1, 2][layer])
                        o = bank(4 + par, rows=NT)
                        for k in range(kinds):
                            at = slice(k * NT, k * NT + NT)
                            mm(o[:, 0:cols], g_lo[:, par, at], mix_at(layer, k, 0, P, 0, cols), start=(k == 0), stop=False, skip_group_check=True)
                            last = mm(o[:, 0:cols], g_hi[:, par, at], mix_at(layer, k, P, V, 0, cols), start=False,
                                      stop=(k == kinds - 1), skip_group_check=True)
                        if layer in (0, 2):
                            last = linear(o[:, F:2 * F], h_t[:, par, :], *own_rows(layer), False)
                        if layer == 1:
                            last = linear(o[:, 0:cols], h_t[:, par, :], *own_rows(layer), False)
                        last.then_inc(n_mixed, 1)
                    if layer == 3 and has(-1):
                        pe.wait_ge(n_agg_copied, t)
                        if has(-2):
                            pe.wait_ge(n_gated, t - 1 + NTILES)
                        linear(bank(7, 0, F, NT), agg_t, *own_rows(layer), True).then_inc(n_out, 1)

                tiles(pe, mixing)
                meet_trio(pe, MIX_END[layer])
                if layer in (0, 2):
                    half = NTILES * (layer // 2)

                    def products(t, par, has):
                        if not has(0):
                            return
                        pe.wait_ge(b_staged, t + (half + 1))
                        if has(-1):
                            pe.wait_ge(b_pairs_copied, t + half)
                        tr(bank(6, 0, NT), b_h[0:NT, par, 0:P], ident[0:NT, 0:NT])
                        tr(bank(6, NT, 2 * NT, S), b_agg[0:NT, par, 0:S], ident[0:NT, 0:NT]).then_inc(b_turned, 1)
                        pe.wait_ge(b_copied, t + (half + 1))
                        rows_t, sums_t = b_t[:, par, 0:NT], b_t[:, par, NT:2 * NT]
                        for c in range(6):
                            if has(-1) or c >= 2:
                                pe.wait_ge(b_used, t * 6 + (6 * half + c - 1))
                            for d in range(2):
                                lhs, rhs = (sums_t, w_ss[0:S, (2 * c + d) * BANK:(2 * c + d + 1) * BANK]) if c < 4 else \
                                    ((rows_t, w_sv) if c == 4 else (sums_t, w_vs))
                                if c >= 4:
                                    rhs = rhs[0:S, d * BANK:d * BANK + BANK]
                                last = mm(bank(2 + 2 * (c % 2) + d, rows=NT), lhs, rhs, start=True, stop=True)
                            last.then_inc(b_chunk, 1)
                        pe.wait_ge(b_pairs, t + (half + 1))
                        for c in range(8):
                            last = tr(bank(6 + c // 4, (c % 4) * NT, (c % 4) * NT + NT), pairs_vv[0:NT, c * P:c * P + P], ident[0:NT, 0:NT])
                        last.then_inc(b_pairs_turned, 1)
                        if has(-2):
                            pe.wait_ge(b_fin, t - 1 + half)
                        pe.wait_ge(b_pairs_copied, t + (half + 1))
                        upd = bank(par, rows=NT)
                        for c in range(8):
                            mm(upd[:, 0:S], pairs_t[:, c * NT:c * NT + NT], w_vv[:, c * S:c * S + S],
                               start=(c == 0), stop=False, skip_group_check=True)
                        pe.wait_ge(b_used, t * 6 + (6 * half + 6))
                        for u in range(V):
                            last = mm(upd[:, S:F], ident[0:NT, 0:NT], prod_vs[0:NT, u * 96:u * 96 + 96], start=False,
                                      stop=(u == V - 1), skip_group_check=True)
                        last.then_inc(b_upd, 1)

                    tiles(pe, products)
                    meet_trio(pe, PROD_END[layer])

        @block.vector
        def _(dve):
            step = Steps(dve, v_step)
            tt, ts, stt = nc.vector.tensor_tensor, nc.vector.tensor_scalar, nc.vector.scalar_tensor_tensor
            cp = nc.vector.tensor_copy
            f3 = fill.rearrange("p (n r) -> p n r", r=REC_D)
            step(nc.vector.memset(small[:, :], 0.0))
            step(nc.vector.memset(fill, 0.0))
            nc.vector.memset(f3[:, :, 1:2], -1.0).then_inc(fill_ready, 1)
            f3 = fill_s.rearrange("p (n r) -> p n r", r=REC_S)
            step(nc.vector.memset(fill_s, 0.0))
            nc.vector.memset(f3[:, :, 1:2], -1.0).then_inc(fill_ready, 1)
            step(nc.vector.memset(zero, 0.0))
            dve.wait_ge(loaded, 64)
            dve.wait_ge(consts_ready, 7)
            for k in range(2):
                step(cp(temp_f, key[k]))
                step(ts(temp_i, temp_f, -12.0, 1.0 / NB, ALU.add, ALU.mult))
                step(cp(blk, temp_i))
                step(stt(loc[k], blk, -float(NB), temp_f, ALU.mult, ALU.add))
                step(ts(temp_f, loc[k], float(NB), None, ALU.is_ge))
                step(ts(slot_of, loc[k], 0.0, None, ALU.is_lt))
                step(tt(temp_f, temp_f, slot_of, ALU.subtract))
                step(tt(blk, blk, temp_f, ALU.add))
                step(stt(loc[k], temp_f, -float(NB), loc[k], ALU.mult, ALU.add))

                def buckets(quad, s, base, used):
                    if used is not None:
                        dve.wait_ge(in_used, used)
                    tt(in_b[:, s], repeat(blk.rearrange("p (q c) -> p q c", q=4)[:, :, bass.ds(quad, 1)], 2, BUCKETS),
                       repeat(iota_row[:, 0:BUCKETS].rearrange("p (o b) -> p o b", o=1), 1, 4), ALU.is_equal).then_inc(in_ready, 1)

                base = 2 * k * QUADS

                def count(i, first, last):
                    for s in range(4):
                        buckets(i * 4 + s, s, base, None if first and k == 0 else i * 4 + (base + s - 3))

                turns(dve, QUADS // 4, count)
                dve.wait_ge(in_used, base + QUADS)
                step(nc.vector.tensor_reduce(total, bank(0, 0, 4 * BUCKETS).rearrange("p (q b) -> p b q", q=4), AX_X, ALU.add))
                step(ts(total_i, total, float(P - 1), None, ALU.add))
                step(ts(total_i, total_i, 7, None, ALU.logical_shift_right))
                step(cp(tiles_in, total_i))
                step(nc.vector.tensor_tensor_scan(ends, tiles_in, zero, 0.0, ALU.add, ALU.add))
                step(tt(start[:, 0], ends, tiles_in, ALU.subtract))
                step(nc.vector.memset(start[:, 0, BLOCKS:BUCKETS], float(TILES)))
                step(ts(start[:, 0], start[:, 0], float(P), None, ALU.mult))
                for q in range(3):
                    step(tt(start[:, q + 1], start[:, q], bank(0, q * BUCKETS, (q + 1) * BUCKETS), ALU.add))
                dve.engine_nop().then_inc(ends_ready, 1)
                dve.wait_ge(ends_turned, k + 1)
                step(cp(ends_col[0:BLOCKS, :], bank(2, 0, 1, BLOCKS)))
                ts(behind[0:BLOCKS, :], iota_tiles[0:BLOCKS, :], ends_col[0:BLOCKS, :], None, ALU.is_ge).then_inc(behind_ready, 1)
                dve.wait_ge(behind_summed, k + 1)
                for c in range(2):
                    step(ts([offs_src, offs_dst][k][0:1, c * (TILES // 2):(c + 1) * (TILES // 2)], bank(3 + c, 0, TILES // 2, 1),
                            float(BLOCKS - 1), float(F), ALU.min, ALU.mult))
                base += QUADS

                buckets(0, 0, base, base)
                buckets(1, 1, base, base)

                def slots_of(i, first, last):
                    for s in range(4):
                        if not (first and s == 0):
                            dve.wait_ge(v_step, i * 4 + (step.n + s))
                        dve.wait_ge(ranked, i * 4 + (QUADS * k + s + 1))
                        tt(found.rearrange("p (q b) -> p q b", q=4), bank(1, 0, 4 * BUCKETS).rearrange("p (q b) -> p q b", q=4),
                           in_b[:, s], ALU.mult).then_inc(slots_found, 1)
                        if not (last and s >= 2):
                            buckets(i * 4 + (s + 2), (s + 2) % 4, base, i * 4 + (base + s - 1))
                        dve.wait_ge(slots_found, i * 4 + (QUADS * k + s + 1))
                        nc.vector.tensor_reduce(slot_of.rearrange("p (q c) -> p q c", q=4)[:, :, bass.ds(i * 4 + s, 1)],
                                                found.rearrange("p (q o b) -> p q o b", q=4, o=1),
                                                AX_X, ALU.add).then_inc(v_step, 1)

                turns(dve, QUADS // 4, slots_of)
                step.n += QUADS
                dve.wait_ge(v_step, step.n)
                step(cp(temp_i, slot_of))
                step(ts(temp_j, temp_i, P - 1, None, ALU.bitwise_and))
                step(ts(temp_i, temp_i, 7, None, ALU.logical_shift_right))
                step(ts(temp_j, temp_j, float(ROW), None, ALU.mult))
                tt(addr[k], temp_i, temp_j, ALU.add).then_inc(addr_ready, 1)
                dve.wait_ge(addr_ready, k + 1)

            x3 = x[0:NT, :].rearrange("p (b f) -> p b f", f=F)
            h3 = h[0:NT, :].rearrange("p (b f) -> p b f", f=F)
            mean_, var_ = mean[0:NT, :], var[0:NT, :]

            def spread(t):
                return repeat(t.rearrange("p (b o) -> p b o", o=1), 2, F)

            for s in range(2):
                dve.wait_ge(chunk_scattered[s], COLS * 8)
            for layer in range(4):
                nc.vector.memset(mix[:, :], 0.0).then_inc(mix_zeroed, 1)
                step(nc.vector.tensor_reduce(mean_, x3, AX_X, ALU.add))
                step(ts(mean_, mean_, 1.0 / F, None, ALU.mult))
                tt(h3, x3, spread(mean_), ALU.subtract).then_inc(centred, 1)
                dve.wait_ge(squared, layer + 1)
                step(nc.vector.tensor_reduce(var_, square[0:NT, :].rearrange("p (b f) -> p b f", f=F), AX_X, ALU.add))
                ts(var_, var_, 1.0 / F, 1e-5, ALU.mult, ALU.add).then_inc(var_ready, 1)
                dve.wait_ge(root_ready, layer + 1)
                step(nc.vector.reciprocal(mean_, var_))
                step(tt(h3, h3, spread(mean_), ALU.mult))
                ts(h[0:NT, :], h[0:NT, :], 0.0, None, ALU.max).then_inc(normed, 1)
                if layer != 1:
                    dve.drain().then_inc(rows_ready, 1)
                meet_all(dve, norm_end(layer))
                step(nc.vector.memset(sums[:, :], 0.0))
                rec = rec_s if layer % 2 == 0 else rec_d
                offs = offs_src if layer % 2 == 0 else offs_dst
                kinds, wide = KINDS[layer], WIDE[layer]
                high = kinds * wide
                base_eq = GROUPS * layer

                lag = 2 if layer == 1 else 1

                def places(i, lo, n):
                    _, at = nc.values_load_multi_w_load_instructions(
                        offs[0:1, bass.ds(i * (SLOTS * GROUP) + GROUP * lo, n * GROUP)], engines=[mybir.EngineType.DVE],
                        min_val=0, max_val=(BLOCKS - 1) * F)
                    return {lo + k // GROUP: at[k:k + GROUP] for k in range(0, n * GROUP, GROUP)}

                def add(i, s, t, first, where):
                    nth = GROUP * s + t
                    if t == 0:
                        dve.wait_ge(scattered, i * SLOTS + (GROUPS * layer + s + 1))
                    blk_sums = sums[0:high, bass.ds(where[s][t], F)]
                    if not (first and nth == 0 and layer == 0):
                        dve.wait_ge(added, i * (SLOTS * GROUP) + (TILES * layer + nth))
                    o = bank(2 * (s % 2) + t // 2, F * (t % 2), F * (t % 2) + F, high)
                    tt(blk_sums, blk_sums, o, ALU.add).then_inc(added, 1)

                def edges(i, first, last_turn):
                    where = places(i, 0, SLOTS - lag) if first else places(i, -lag, SLOTS)
                    for s in range(SLOTS):
                        dve.wait_ge(x_ready[s], i * 64 + 64 * (TURNS * layer + 1))
                        if not (first and s < 2 and layer == 0):
                            dve.wait_ge(scattered, i * SLOTS + (GROUPS * layer + s - 1))
                        hs = hot[:, s % 2, :, 0:high].rearrange("p t (k n) -> p t k n", k=kinds)
                        eq = hs[:, :, 4, :] if kinds == 5 else one_hot[:, s % 2, :, 0:wide]
                        tt(eq, repeat(rec[:, s, :, 1:2], 2, wide),
                           repeat(iota_row[:, 0:wide].rearrange("p (o n) -> p o n", o=1), 1, GROUP), ALU.is_equal).then_inc(eq_ready, 1)
                        dve.wait_ge(eq_ready, i * SLOTS + (base_eq + s + 1))
                        hot_op = tt(hs[:, :, 0:4, :], repeat(eq.rearrange("p t (o n) -> p t o n", o=1), 2, 4),
                                    repeat(rec[:, s, :, 2:6].rearrange("p t (k o) -> p t k o", o=1), 3, wide), ALU.mult)
                        if layer != 1:
                            hot_op.then_inc(hot_ready, 1)
                        adds = not (first and s < lag)
                        if adds and layer != 1:
                            for t in range(GROUP):
                                add(i, s - lag, t, first, where)
                        if layer == 1:
                            dve.wait_ge(w_ready, i * SLOTS + (s + 1))
                            wps = psum[:, 6 * BANK:8 * BANK].rearrange("p (t c) -> p t c", t=GROUP)
                            r = rows_x[:, s, :, :]
                            m = msg[:, s % 2, :, :]
                            rv = r[:, :, S:F].rearrange("p t (c n) -> p t c n", n=V)
                            pieces = m[:, :, S + F:MSG].rearrange("p t (q n) -> p t q n", n=V)

                            def weigh(o, rows, lo, n):
                                return tt(o, rows, repeat(wps[:, :, lo:lo + V].rearrange("p t (o n) -> p t o n", o=1), 2, n), ALU.mult)

                            tt(m[:, :, 0:S], r[:, :, 0:S], wps[:, :, 0:S], ALU.mult)
                            if adds:
                                add(i, s - lag, 0, first, where)
                            tt(m[:, :, F:F + S], r[:, :, 0:S], wps[:, :, S:2 * S], ALU.mult)
                            if adds:
                                add(i, s - lag, 1, first, where)
                            weigh(m[:, :, S:F].rearrange("p t (c n) -> p t c n", n=V), rv, 128, 3)
                            if adds:
                                add(i, s - lag, 2, first, where)
                            weigh(pieces[:, :, 0:1, :], rv[:, :, 0:1, :], 160, 1)
                            weigh(pieces[:, :, 4:6, :], rv[:, :, 1:3, :], 160, 2)
                            weigh(pieces[:, :, 1:3, :], rv[:, :, 1:3, :], 192, 2)
                            weigh(pieces[:, :, 3:4, :], rv[:, :, 0:1, :], 192, 1).then_inc(msg_ready, 1)
                            if adds:
                                add(i, s - lag, 3, first, where)

                turns(dve, TURNS, edges)
                where = places(TURNS, -lag, lag)
                for s in range(-lag, 0):
                    for t in range(GROUP):
                        add(TURNS, s, t, False, where)
                meet_all(dve, edge_end(layer))
                base = NTILES * layer

                def mixing(t, par, has):
                    if has(0):
                        dve.wait_ge(n_turned, t + (base + 1))
                        if has(-2):
                            dve.wait_ge(n_mixed, t + (base - 1))
                        for lo, n, b in ((0, PER - 1, 0), (PER - 1, 1, 1)):
                            cp(g_lo[:, par, 0:kinds * NT].rearrange("p (k j n) -> p k j n", k=kinds, n=NB)[:, :, lo:lo + n, :],
                               bank(b, 0, n * high).rearrange("p (j k n) -> p k j n", k=kinds, n=wide)[:, :, :, 0:NB])
                        cp(h_t[:, par, 0:NT], bank(1, P, P + NT)).then_inc(n_low, 1)
                    if has(-1) and layer != 3:
                        o = bank(4 + (1 - par), rows=NT)
                        hb = h[0:NT, bass.ds((t - 1) * F, F)]
                        xb = x[0:NT, bass.ds((t - 1) * F, F)]
                        if layer in (0, 2):
                            half = NTILES * (layer // 2)
                            dve.wait_ge(n_agg, t + half)
                            tt(fin[0:NT, 0:F], hb, fin[0:NT, 0:F], ALU.add).then_inc(n_scaled, 1)
                            dve.wait_ge(n_scaled, t + (0 if layer == 0 else 2 * NTILES))
                            tt(xb, xb, fin[0:NT, 0:F], ALU.add).then_inc(n_done, 1)
                        if layer == 1:
                            dve.wait_ge(n_mixed, t + base)
                            if has(-2):
                                dve.wait_ge(n_done, t - 1 + base)
                            tt(fin[0:NT, :], o[:, 0:192], repeat(scale_a[0:NT, bass.ds(t - 1, 1)], 1, 192), ALU.mult).then_inc(n_fin, 1)
                            dve.wait_ge(n_gated, t)
                            vecs = three(fin[0:NT, 96:192])
                            tt(vecs, vecs, repeat(gate[0:NT, S:96].rearrange("p (o n) -> p o n", o=1), 1, 3), ALU.mult).then_inc(n_scaled, 1)
                            xs = x[0:NT, bass.ds((t - 1) * F, S)]
                            xv = x[0:NT, bass.ds((t - 1) * F + S, 96)]
                            tt(xs, xs, gate[0:NT, 0:S], ALU.add)
                            dve.wait_ge(n_scaled, t + NTILES)
                            tt(xv, xv, fin[0:NT, 96:192], ALU.add).then_inc(n_done, 1)
                    if has(-2) and layer == 3:
                        hb = h[0:NT, bass.ds((t - 2) * F, F)]
                        xb = x[0:NT, bass.ds((t - 2) * F, F)]
                        dve.wait_ge(n_gated, t - 1 + NTILES)
                        tt(fin[0:NT, 0:F], hb, relu[0:NT, :], ALU.add).then_inc(n_fin, 1)
                        dve.wait_ge(n_fin, t - 1 + NTILES)
                        tt(xb, xb, fin[0:NT, 0:F], ALU.add).then_inc(n_done, 1)

                tiles(dve, mixing)
                meet_trio(dve, MIX_END[layer])
                if layer in (0, 2):
                    half = NTILES * (layer // 2)

                    def products(t, par, has):
                        if has(0):
                            dve.wait_ge(b_staged, t + (half + 1))
                            if has(-1) and layer == 0:
                                dve.wait_ge(b_pairs_turned, t + half)
                            agg, hr = b_agg[0:NT, par, :], b_h[0:NT, par, :]
                            if layer == 0:
                                vector_pairs(nc.vector, step, t, par)
                            if has(-1):
                                dve.wait_ge(b_summed, (t + half) * 2)
                            for c in range(6):
                                dve.wait_ge(b_chunk, t * 6 + (6 * half + c + 1))
                                part = psum[0:NT, (2 + 2 * (c % 2)) * BANK:(4 + 2 * (c % 2)) * BANK]
                                if c < 4:
                                    tt(prod_ss[0:NT, c * 2 * BANK:(c + 1) * 2 * BANK].rearrange("p (u w) -> p u w", w=S),
                                       part.rearrange("p (u w) -> p u w", w=S),
                                       repeat(hr[:, c * 16:c * 16 + 16].rearrange("p (u o) -> p u o", o=1), 2, S),
                                       ALU.mult).then_inc(b_used, 1)
                                else:
                                    if c == 5 and has(-1):
                                        dve.wait_ge(b_upd, t + half)
                                    by = (agg if c == 4 else hr)[:, S:F].rearrange("p (c u o) -> p u c o", c=3, o=1)
                                    tt((prod_sv if c == 4 else prod_vs)[0:NT, :].rearrange("p (u c n) -> p u c n", u=V, c=3),
                                       repeat(part.rearrange("p (u o n) -> p u o n", u=V, o=1), 2, 3), repeat(by, 3, V),
                                       ALU.mult).then_inc(b_used, 1)
                        if has(-1):
                            red = b_red[0:NT, 1 - par, :]
                            xb = x[0:NT, bass.ds((t - 1) * F, F)]
                            dve.wait_ge(b_upd, t + half)
                            dve.wait_ge(b_summed, (t + half) * 2)
                            tt(red, red, bank(1 - par, 0, F, NT), ALU.add).then_inc(b_fin, 1)
                            dve.wait_ge(b_fin, t + half)
                            tt(xb, xb, red, ALU.add).then_inc(b_done, 1)
                        if has(0):
                            red = b_red[0:NT, par, :]
                            if has(-2):
                                dve.wait_ge(b_done, t - 1 + half)
                            dve.wait_ge(b_used, t * 6 + (6 * half + 6))
                            nc.vector.tensor_reduce(red[:, 0:S], prod_ss[0:NT, :].rearrange("p (u w) -> p w u", w=S),
                                                    AX_X, ALU.add).then_inc(b_summed, 1)
                            nc.vector.tensor_reduce(red[:, S:F], prod_sv[0:NT, :].rearrange("p (u m) -> p m u", m=96),
                                                    AX_X, ALU.add).then_inc(b_summed, 1)

                    tiles(dve, products)
                    if layer == 0:
                        step.n += 4 * NTILES
                    meet_trio(dve, PROD_END[layer])


def kernel(**inputs):
    import numpy as _np
    import concourse.bacc as _bacc
    from concourse import mybir as _mybir
    from concourse.bass_utils import run_bass_kernel_spmd as _run

    arr = {k: _np.asarray(v) for k, v in inputs.items()}

    x = arr["x"]
    vec = x[:, S:].reshape(N, V, C3).transpose(0, 2, 1).reshape(N, C3 * V)
    put = {"x": _np.concatenate([x[:, :S], vec], axis=1),
           "node_vec1": _np.ascontiguousarray(arr["node_vec1"].reshape(NTILES, NT).T)}
    for k in ("src", "dst"):
        o = _np.full((P * COLS,), N, arr[k].dtype)
        o[:E] = arr[k]
        put[k] = o.reshape(P, COLS)
    attrs = _np.zeros((P * COLS, 4 + R_), x.dtype)
    attrs[:E, :4] = arr["edge_attr_4"]
    attrs[:E, 4:] = arr["edge_attr_64"]
    put["attrs"] = attrs.reshape(P, COLS, 4 + R_)
    put["attrs_4"] = _np.ascontiguousarray(attrs[:, :4]).reshape(P, COLS, 4)
    for k, v in arr.items():
        if k[:2] in ("L0", "L1", "L2", "L3"):
            if k[:7] == "L2_gnn_" and k[7:9] == "wm":
                v = v[:, 0, :]
            if k in ("L0_gnn_Wu_vv", "L2_gnn_wu110"):
                v = v.reshape(-1, v.shape[2])
            if k in ("L0_gnn_Wu_sv", "L2_gnn_wu011"):
                v = v.reshape(v.shape[0], -1)
            put[k] = v
    nc = _bacc.Bacc("TRN2", target_bir_lowering=False, num_devices=1)
    arrays, aps = {}, {}
    for name, v in put.items():
        v = _np.ascontiguousarray(v)
        arrays[f"in_{name}"] = v
        aps[name] = nc.dram_tensor(f"in_{name}", v.shape, _mybir.dt.from_np(v.dtype), kind="ExternalInput").ap()
    out = nc.dram_tensor("out_0", (N, F), _mybir.dt.float32, kind="ExternalOutput").ap()
    program(nc, aps, out)
    r = _run(nc, [arrays], core_ids=[0])
    got = r.results[0]["out_0"]
    vec = got[:, S:].reshape(N, C3, V).transpose(0, 2, 1).reshape(N, C3 * V)
    return _np.concatenate([got[:, :S], vec], axis=1)
```
